# Optimizing a Trainium2 kernel written in Bass

```python
import numpy as np
import jax
import jax.numpy as jnp

def _softmax(x, axis=-1):
    return jax.nn.softmax(x, axis=axis)

def _gelu(x):
    return jax.nn.gelu(x, approximate=True)

def _silu(x):
    return jax.nn.silu(x)

def _sigmoid(x):
    return jax.nn.sigmoid(x)

def _layernorm(x, axis=-1, eps=1e-05):
    m = jnp.mean(x, axis=axis, keepdims=True)
    v = jnp.var(x, axis=axis, keepdims=True)
    return (x - m) / jnp.sqrt(v + eps)

def _scatter_add(tgt, idx, src, axis=0):
    return tgt.at[idx].add(src)

def _segment_sum(src, seg, n):
    return jax.ops.segment_sum(src, seg, n)
kernel_name = 'mk_recurrent_d1_jaxref_r8_bebc3c'

def setup_inputs(seed: int=0):
    np.random.seed(seed)
    _w = jnp.asarray

    def _L0_attn_setup():
        import jax, jax.numpy as jnp
        import numpy as np
        B, T, D, DF, K = (4, 256, 128, 2, 7)
        H = D * DF

        def _causal_dwconv(v, w, b):
            lhs = v.transpose(0, 2, 1)
            rhs = w[:, None, :]
            y = jax.lax.conv_general_dilated(lhs, rhs, window_strides=(1,), padding=[(w.shape[-1] - 1, 0)], dimension_numbers=('NCH', 'OIH', 'NCH'), feature_group_count=w.shape[0])
            return y.transpose(0, 2, 1) + b

        def _ssm(v, log_decay, mix_w, mix_b):
            decay = jax.nn.sigmoid(log_decay)
            a = jnp.broadcast_to(decay, v.shape)

            def comb(c1, c2):
                a1, b1 = c1
                a2, b2 = c2
                return (a1 * a2, b1 * a2 + b2)
            _, y = jax.lax.associative_scan(comb, (a, v), axis=1)
            return y @ mix_w + mix_b
        key = jax.random.key(seed)
        ks = jax.random.split(key, 8)
        sc = 0.02
        return {'x': jax.random.normal(ks[0], (B, T, D), jnp.float32), 'norm_gamma': jnp.ones((D,), jnp.float32), 'norm_beta': jnp.zeros((D,), jnp.float32), 'in_w': jax.random.normal(ks[1], (D, 2 * H), jnp.float32) * sc, 'in_b': jnp.zeros((2 * H,), jnp.float32), 'dw_w': jax.random.normal(ks[2], (H, K), jnp.float32) * sc, 'dw_b': jnp.zeros((H,), jnp.float32), 'log_decay': jax.random.normal(ks[3], (H,), jnp.float32), 'mix_w': jax.random.normal(ks[4], (H, H), jnp.float32) * sc, 'mix_b': jnp.zeros((H,), jnp.float32), 'out_w': jax.random.normal(ks[5], (H, D), jnp.float32) * sc, 'out_b': jnp.zeros((D,), jnp.float32)}
    _L0_attn_in = _L0_attn_setup()

    def _L0_ffn_setup():
        import jax, jax.numpy as jnp
        import numpy as np
        D_MODEL = 128
        HIDDEN = 512
        NUM_EXPERTS = 8
        TOP_K = 2
        DEPTH = 12
        DEPTH_SCALE = 1.0 / np.sqrt(DEPTH)
        key = jax.random.key(seed)
        k_x, k_r, k_g, k_u, k_d = jax.random.split(key, 5)
        s_in = 1.0 / np.sqrt(D_MODEL)
        s_hid = 1.0 / np.sqrt(HIDDEN)
        return {'x': jax.random.normal(k_x, (2, 256, D_MODEL), dtype=jnp.float32), 'Wr': jax.random.normal(k_r, (D_MODEL, NUM_EXPERTS), dtype=jnp.float32) * s_in, 'Wg': jax.random.normal(k_g, (NUM_EXPERTS, D_MODEL, HIDDEN), dtype=jnp.float32) * s_in, 'Wu': jax.random.normal(k_u, (NUM_EXPERTS, D_MODEL, HIDDEN), dtype=jnp.float32) * s_in, 'Wd': jax.random.normal(k_d, (NUM_EXPERTS, HIDDEN, D_MODEL), dtype=jnp.float32) * s_hid}
    _L0_ffn_in = _L0_ffn_setup()
    _d = {'L0_attn_x': _L0_attn_in['x'], 'L0_attn_norm_gamma': _L0_attn_in['norm_gamma'], 'L0_attn_norm_beta': _L0_attn_in['norm_beta'], 'L0_attn_in_w': _L0_attn_in['in_w'], 'L0_attn_in_b': _L0_attn_in['in_b'], 'L0_attn_dw_w': _L0_attn_in['dw_w'], 'L0_attn_dw_b': _L0_attn_in['dw_b'], 'L0_attn_log_decay': _L0_attn_in['log_decay'], 'L0_attn_mix_w': _L0_attn_in['mix_w'], 'L0_attn_mix_b': _L0_attn_in['mix_b'], 'L0_attn_out_w': _L0_attn_in['out_w'], 'L0_attn_out_b': _L0_attn_in['out_b'], 'L0_ffn_Wr': _L0_ffn_in['Wr'], 'L0_ffn_Wg': _L0_ffn_in['Wg'], 'L0_ffn_Wu': _L0_ffn_in['Wu'], 'L0_ffn_Wd': _L0_ffn_in['Wd']}
    _x0 = _d['L0_attn_x']
    _d['L0_attn_x'] = jax.random.normal(jax.random.fold_in(jax.random.key(seed), 1), (16, 512, 128), dtype=_x0.dtype)
    del _x0
    return _d

def reference(L0_attn_x, L0_attn_norm_gamma, L0_attn_norm_beta, L0_attn_in_w, L0_attn_in_b, L0_attn_dw_w, L0_attn_dw_b, L0_attn_log_decay, L0_attn_mix_w, L0_attn_mix_b, L0_attn_out_w, L0_attn_out_b, L0_ffn_Wr, L0_ffn_Wg, L0_ffn_Wu, L0_ffn_Wd):

    def _L0_attn_ref(x, norm_gamma, norm_beta, in_w, in_b, dw_w, dw_b, log_decay, mix_w, mix_b, out_w, out_b):
        import jax, jax.numpy as jnp
        import numpy as np
        B, T, D, DF, K = (4, 256, 128, 2, 7)
        H = D * DF

        def _causal_dwconv(v, w, b):
            lhs = v.transpose(0, 2, 1)
            rhs = w[:, None, :]
            y = jax.lax.conv_general_dilated(lhs, rhs, window_strides=(1,), padding=[(w.shape[-1] - 1, 0)], dimension_numbers=('NCH', 'OIH', 'NCH'), feature_group_count=w.shape[0])
            return y.transpose(0, 2, 1) + b

        def _ssm(v, log_decay, mix_w, mix_b):
            decay = jax.nn.sigmoid(log_decay)
            a = jnp.broadcast_to(decay, v.shape)

            def comb(c1, c2):
                a1, b1 = c1
                a2, b2 = c2
                return (a1 * a2, b1 * a2 + b2)
            _, y = jax.lax.associative_scan(comb, (a, v), axis=1)
            return y @ mix_w + mix_b
        res = x
        mu = x.mean(-1, keepdims=True)
        var = x.var(-1, keepdims=True)
        xn = (x - mu) * jax.lax.rsqrt(var + 1e-05) * norm_gamma + norm_beta
        u = xn @ in_w + in_b
        g, v = jnp.split(u, 2, axis=-1)
        g = jax.nn.sigmoid(g)
        v = _causal_dwconv(v, dw_w, dw_b) + _ssm(v, log_decay, mix_w, mix_b)
        y = g * v @ out_w + out_b
        return res + y

    def _L0_ffn_ref(x, Wr, Wg, Wu, Wd):
        import jax, jax.numpy as jnp
        import numpy as np
        D_MODEL = 128
        HIDDEN = 512
        NUM_EXPERTS = 8
        TOP_K = 2
        DEPTH = 12
        DEPTH_SCALE = 1.0 / np.sqrt(DEPTH)
        B, T, C = x.shape
        flat_x = x.reshape(-1, C)
        logits = flat_x @ Wr
        top_vals, top_idx = jax.lax.top_k(logits, TOP_K)
        rw = jax.nn.softmax(top_vals.astype(jnp.float32), axis=-1).astype(x.dtype)
        combine = jnp.sum(rw[..., None] * jax.nn.one_hot(top_idx, NUM_EXPERTS, dtype=x.dtype), axis=1)
        g = jnp.einsum('nc,ech->neh', flat_x, Wg)
        u = jnp.einsum('nc,ech->neh', flat_x, Wu)
        h = jax.nn.silu(g) * u
        eo = jnp.einsum('neh,ehc->nec', h, Wd) * DEPTH_SCALE
        out = jnp.einsum('ne,nec->nc', combine, eo)
        return out.reshape(B, T, C)
    x = L0_attn_x
    xn = _layernorm(x, axis=-1)
    s = _L0_attn_ref(xn, L0_attn_norm_gamma, L0_attn_norm_beta, L0_attn_in_w, L0_attn_in_b, L0_attn_dw_w, L0_attn_dw_b, L0_attn_log_decay, L0_attn_mix_w, L0_attn_mix_b, L0_attn_out_w, L0_attn_out_b)
    g = _silu(_L0_ffn_ref(xn, L0_ffn_Wr, L0_ffn_Wg, L0_ffn_Wu, L0_ffn_Wd))
    x = x + s * g
    return x

_drawn_inputs = setup_inputs


def setup_inputs(seed=0):
    import zlib

    import numpy as np

    out = dict(_drawn_inputs(seed))
    spreads = {'L0_attn_norm_gamma': (1.0, 0.6),
     'L0_attn_norm_beta': (0.0, 0.8),
     'L0_attn_in_b': (0.0, 0.8),
     'L0_attn_dw_b': (0.0, 2.0),
     'L0_attn_mix_b': (0.0, 2.0),
     'L0_attn_out_b': (0.0, 2.0)}
    factors = {'L0_attn_in_w': 8.0,
     'L0_attn_dw_w': 171.409,
     'L0_attn_log_decay': 8.0,
     'L0_attn_mix_w': 8.0,
     'L0_attn_out_w': 8.0}
    for name, (base, spread) in spreads.items():
        noise = np.random.default_rng([zlib.crc32(name.encode()), seed]).standard_normal(out[name].shape)
        drawn = base * np.exp(spread * noise) if base else spread * noise
        out[name] = jnp.asarray(drawn.astype(out[name].dtype))
    for name, factor in factors.items():
        out[name] = (out[name] * factor).astype(out[name].dtype)
    return out
```

```python
import concourse.bass as bass
from concourse import mybir
from contextlib import ExitStack


def recurrent_moe_block(nc, x, gamma, beta, in_w, in_b, dw_w, dw_b, log_decay, mix_w, mix_b,
                        out_w, out_b, w_route, w_gate, w_up, w_down, out):
    F32, F32R, I32, U32 = mybir.dt.float32, mybir.dt.float32r, mybir.dt.int32, mybir.dt.uint32
    ALU, ACT, AX = mybir.AluOpType, mybir.ActivationFunctionType, mybir.AxisListType

    P = 128
    B, T, D = x.shape
    H = in_w.shape[1] // 2
    K = dw_w.shape[1]
    E, _, HID = w_gate.shape
    TOPK = 2
    PAD = K - 1
    CB = H // P
    HB = HID // P
    S = T // P
    NS = B * S
    GROUPS = 2
    BG, SG = B // GROUPS, NS // GROUPS
    QT = 4
    NT = -(-(SG * TOPK + E - 1) // 8) * 8
    NQ = NT // QT
    TILES = GROUPS * NT
    EPS = 1e-5
    DEPTH_SCALE = 1.0 / (12 ** 0.5)
    HEAD = 5
    RING = 4

    x_v = x.rearrange("b (j p) d -> b p j d", p=P)
    out_v = out.rearrange("b (j p) d -> b p j d", p=P)
    sorted_x = [nc.dram_tensor(f"sorted_x{g}", [NT * P, D], F32, kind="Internal").ap()
                for g in range(GROUPS)]
    sorted_y = [nc.dram_tensor(f"sorted_y{g}", [NT * P, D], F32, kind="Internal").ap()
                for g in range(GROUPS)]
    sx_v = [v.rearrange("(q p s) d -> q p (s d)", p=P, s=QT) for v in sorted_x]
    sy_v = [v.rearrange("(q p s) d -> q p (s d)", p=P, s=QT) for v in sorted_y]

    ctx = ExitStack()
    with ctx:
        def sb(name, shape, dt=F32):
            return ctx.enter_context(nc.sbuf_tensor(name, shape, dt))

        def sem(name):
            return ctx.enter_context(nc.semaphore(name))

        xn = sb("xn", [P, NS * D])
        gu_w = sb("gu_w", [P, E * 2 * 2 * HID], F32R)
        dn_w = sb("dn_w", [P, E * 2 * HB * D], F32R)
        inw = sb("inw", [P, 2, 2 * H], F32R)
        mixw = sb("mixw", [P, 2, CB, H], F32R)
        outw = sb("outw", [P, 2, CB, D], F32R)
        outb = sb("outb", [1, 3, D], F32R)
        ident = sb("ident", [P, P])
        route_w = sb("route_w", [P, E])
        logits = sb("logits", [P, NS * E])
        rows = sb("rows", [P, TOPK, NS], U32)
        rw = sb("rw", [P, TOPK, NS])
        tile_expert = sb("tile_expert", [P, TILES], I32)
        var_n = sb("var_n", [P, NS])
        params = sb("params", [P, 64])
        gamma_c, beta_c = params[:, 0:1], params[:, 1:2]
        inb_c, bias_c = params[:, 2:6], params[:, 6:10]
        dww_c = params[:, 10:10 + CB * K]
        dwb_c, mixb_c, addb_c = params[:, 24:26], params[:, 26:28], params[:, 28:30]
        ld_c, decay_c = params[:, 30:32], params[:, 32:34]
        ramp = params[:, 34:42]
        ones_f = params[:, 42:43]
        minus1 = params[:, 43:44]
        outb_f = sb("outb_f", [1, D])
        work = sb("work", [P, 6 * HID])
        stage = work[:, :].rearrange("p (r n) -> p r n", r=2)
        silu_h = work[:, 0:2 * HID].rearrange("p (r n) -> p r n", r=2)
        x_quad = work[:, 2 * HID:4 * HID].rearrange("p (r n) -> p r n", r=2)
        y_quad = work[:, 4 * HID:6 * HID].rearrange("p (r n) -> p r n", r=2)
        gate = work[:, 0:2 * HID].rearrange("p (c t) -> p c t", c=CB)
        xhl = sb("xhl", [P, 2, 2, P], F32R)
        hhl = sb("hhl", [P, 2, 2, HID], F32R)
        zhl = sb("zhl", [P, 2, T], F32R)
        vpad = sb("vpad", [P, CB, PAD + T])
        acc = sb("acc", [P, CB * T])
        chl = sb("chl", [P, 2, CB, T], F32R)
        xr = sb("xr", [P, 2 * T])
        x_back = xr[:, 0:T]
        z = xr[:, T:2 * T]
        x_in = [xr[:, :], acc[:, :]]
        xn_t = [vpad[:, 0, 0:T], vpad[:, 1, 0:T]]
        tri = zhl[:, 0, 0:P]
        ones_r = zhl[:, 0, P:2 * P]
        picked = chl[:, 0, 0, 0:SG * E]
        ga = sb("ga", [P, RING * S * TOPK * D])
        at = [0]

        def scratch(*shape):
            n = 1
            for s in shape:
                n *= s
            v = ga[:, at[0]:at[0] + n]
            at[0] += n
            assert at[0] <= RING * S * TOPK * D
            return v if len(shape) == 1 else v.rearrange("p (a b) -> p a b", a=shape[0])

        inw_raw, mixw_raw, outw_raw = scratch(2 * H), scratch(CB * H), scratch(CB * D)
        tri_f = scratch(2 * P)
        same, first_e, second_e, rest = (scratch(SG, E) for _ in range(4))
        max1, max2, code_max, gap = (scratch(SG) for _ in range(4))
        running, before = (scratch(E, SG) for _ in range(2))
        per_tile = rest.rearrange("p t e -> p (t e)").rearrange("p (e t) -> p e t", e=E)
        place = running
        n_e, tiles_e, ends_e, base_e = (scratch(E) for _ in range(4))
        tile_no = scratch(NT)
        past = scratch(NT, E)
        n_past = tile_no
        small = sb("small", [P, 2 * S * 8 + 6 * 2 * S])
        stats = small[:, 0:48].rearrange("p (j k) -> p j k", k=6)
        meanvar = small[:, 48:64].rearrange("p (k j) -> p k j", k=2)
        var_eps, std, rstd, newton = (small[:, 64 + 8 * k:72 + 8 * k] for k in range(4))
        ints = sb("ints", [P, 4 * SG], I32)

        banks = [ctx.enter_context(nc.psum_tensor(f"bank{k}", [P, 512], F32)) for k in range(8)]

        s_params = sem("params_loaded")
        s_mixraw = sem("mixer_weights_loaded")
        s_x = [sem("x_loaded_0"), sem("x_loaded_1")]
        s_const = sem("constants_built")
        s_tri = sem("triangle_built")
        s_dconst = sem("vector_constants")
        s_zero = sem("zeros_built")
        s_zeroed = sem("sorted_x_zeroed")
        s_w = [sem("expert_loaded_0"), sem("expert_loaded_1")]
        s_whi = sem("expert_hi")
        s_wlo = sem("expert_lo")
        s_n = sem("norm_steps")
        s_var = sem("variance_ready")
        s_std = sem("std_ready")
        s_xnr = sem("xn_ready")
        s_xnc = sem("xn_kept")
        s_xt = sem("xn_transposed")
        s_xte = sem("xn_t_ready")
        s_lg = sem("logits_summed")
        s_lge = sem("logits_ready")
        s_r = sem("route_steps")
        s_pick = sem("experts_picked")
        s_cnt = sem("pairs_counted")
        s_gap = sem("logit_gap")
        s_sig = sem("expert_weights")
        s_nv = sem("xn_variance_eps")
        s_nsd = sem("xn_std")
        s_place = sem("places_ready")
        s_sc = [sem("scatter_even"), sem("scatter_odd")]
        s_scb = sem("batches_scattered")
        s_prep = sem("prep_steps")
        s_bmm = sem("bias_product")
        s_dec = sem("decay_ready")
        s_mw = sem("mixer_weights_ready")
        s_q = [sem("x_quad_loaded_0"), sem("x_quad_loaded_1")]
        s_fx = sem("tile_transposed")
        s_fxh = sem("tile_hi")
        s_fxl = sem("tile_lo")
        s_fg = sem("gate_product")
        s_fu = sem("up_product")
        s_fs = sem("silu_ready")
        s_fh = sem("hidden_ready")
        s_ft = sem("hidden_transposed")
        s_fhh = sem("hidden_hi")
        s_fhl = sem("hidden_lo")
        s_fy = sem("down_product")
        s_fye = sem("y_ready")
        s_yst = [sem("y_quad_stored_0"), sem("y_quad_stored_1")]
        s_z = sem("z_ready")
        s_zt = sem("z_transposed")
        s_zh = sem("z_hi")
        s_zl = sem("z_lo")
        s_v = sem("v_product")
        s_g = sem("g_product")
        s_ve = sem("v_ready")
        s_ge = sem("gate_ready")
        s_t0 = sem("first_tap")
        s_c = sem("mixer_steps")
        s_y = sem("state_ready")
        s_yh = sem("state_hi")
        s_yl = sem("state_lo")
        s_mx = sem("mix_product")
        s_gv = sem("gated_sum")
        s_gvh = sem("gated_hi")
        s_gvl = sem("gated_lo")
        s_o = sem("out_product")
        s_s = sem("s_ready")
        s_gt = [sem("gather_even"), sem("gather_odd")]
        s_gtb = sem("batches_gathered")
        s_xb = sem("x_back_loaded")
        s_f = sem("combine_steps")
        s_fc = sem("ffn_combined")
        s_fsi = sem("ffn_silu")
        s_fin = sem("result_ready")
        s_out = sem("result_stored")

        block = ctx.enter_context(nc.Block())

        class Linked:

            def __init__(self, engine, counter):
                self.engine, self.counter, self.base, self.n = engine, counter, 0, 0

            def __call__(self, instruction, wait=True):
                self.n += 1
                instruction.then_inc(self.counter, 1)
                if wait:
                    self.engine.wait_ge(self.counter, self.base + self.n)

        XW = 2 * S
        NORM_STEPS = B // 2
        GW = SG * E

        def experts_schedule(first, step, last):
            for k in range(8):
                step(k, k, True)
            with first(1, TILES // 8 - 1) as it:
                for k in range(8):
                    step(it * 8 + k, k, False)
            for k in range(8):
                step(TILES - 8 + k, k, True)
            for k in range(last):
                step(TILES + k, k, True)

        @block.sync
        def _(sp):
            def load_x(step_, par):
                for h in range(2):
                    sp.dma_start(x_in[par].rearrange("p (h j d) -> p h j d", h=2, d=D)[:, h],
                                 x_v[bass.ds(2 * step_ + h, 1)].rearrange("a p j d -> (a p) j d")
                                 ).then_inc(s_x[par], 16)

            load_x(0, 0)
            for dst, src in ((route_w[:, :], w_route),
                             (gamma_c, gamma.rearrange("(p a) -> p a", a=1)),
                             (beta_c, beta.rearrange("(p a) -> p a", a=1)),
                             (inb_c, in_b.rearrange("(c p) -> p c", p=P)),
                             (dww_c.rearrange("p (c k) -> p c k", c=CB),
                              dw_w.rearrange("(c p) k -> p c k", p=P)),
                             (dwb_c, dw_b.rearrange("(c p) -> p c", p=P)),
                             (mixb_c, mix_b.rearrange("(c p) -> p c", p=P)),
                             (ld_c, log_decay.rearrange("(c p) -> p c", p=P)),
                             (outb_f[:, :], out_b.rearrange("(a d) -> a d", a=1))):
                with nc.allow_non_contiguous_dma(reason="a few small parameters"):
                    sp.dma_start(dst, src).then_inc(s_params, 16)
            sp.dma_start(inw_raw, in_w).then_inc(s_mixraw, 16)
            sp.dma_start(mixw_raw.rearrange("p (c n) -> p c n", c=CB),
                         mix_w.rearrange("(c p) n -> p c n", p=P)).then_inc(s_mixraw, 16)
            sp.dma_start(outw_raw.rearrange("p (c n) -> p c n", c=CB),
                         out_w.rearrange("(c p) n -> p c n", p=P)).then_inc(s_mixraw, 16)
            load_x(1, 1)
            sp.wait_ge(s_zero, 1)
            zeros = hhl[:, 0, 0, :].bitcast(F32)
            for g in range(GROUPS):
                sp.dma_start(sx_v[g].rearrange("q p n -> p q n"),
                             zeros.rearrange("p (a n) -> p a n", a=1).to_broadcast([P, NQ, HID])
                             ).then_inc(s_zeroed, 16)
            with sp.Fori(1, NORM_STEPS // 2) as it:
                for par in range(2):
                    transposed = sp.snap(4 * it + 2 * par - 2)
                    sp.wait_ge(s_xnc, 2 * it + par - 1)
                    sp.wait_ge(s_xt, transposed)
                    load_x(2 * it + par, par)

            def quad_in(g, q, slot, reuse):
                if reuse:
                    sp.wait_ge(s_fx, (g * NQ + q - 1) * QT)
                sp.dma_start(x_quad[:, slot, :],
                             sx_v[g][bass.ds(q, 1)].rearrange("a p n -> (a p) n")
                             ).then_inc(s_q[slot], 16)

            def quad_out(g, q, slot):
                sp.wait_ge(s_fye, (g * NQ + q + 1) * QT)
                sp.dma_start(sy_v[g][bass.ds(q, 1)].rearrange("a p n -> (a p) n"),
                             y_quad[:, slot, :]).then_inc(s_yst[slot], 16)

            sp.wait_ge(s_wlo, 2 * E)
            for g in range(GROUPS):
                sp.wait_ge(s_scb, (g + 1) * BG)
                for slot in range(2):
                    quad_in(g, slot, slot, g > 0)
                    if g:
                        quad_out(g - 1, NQ - 2 + slot, slot)
                with sp.Fori(1, NQ // 2) as it:
                    for slot in range(2):
                        quad_in(g, 2 * it + slot, slot, True)
                        quad_out(g, 2 * it + slot - 2, slot)
            for slot in range(2):
                quad_out(GROUPS - 1, NQ - 2 + slot, slot)

            def batch_in(b):
                sp.dma_start(x_back.rearrange("p (j d) -> p j d", d=D),
                             x_v[bass.ds(b, 1)].rearrange("a p j d -> (a p) j d")
                             ).then_inc(s_xb, 16)

            def batch_out(b):
                sp.wait_ge(s_fin, b + 1)
                sp.dma_start(out_v[bass.ds(b, 1)].rearrange("a p j d -> (a p) j d"),
                             x_back.rearrange("p (j d) -> p j d", d=D)).then_inc(s_out, 16)

            batch_in(0)
            with sp.Fori(1, B) as b:
                batch_out(b - 1)
                sp.wait_ge(s_out, 16 * b)
                batch_in(b)
            batch_out(B - 1)
            sp.wait_ge(s_out, 16 * B)

        @block.gpsimd
        def _(pool):
            nc.gpsimd.memset(hhl[:, 0, 0, :].bitcast(F32), 0.0
                             ).then_inc(s_zero, 1)
            nc.gpsimd.memset(ident[:, :], 0.0).then_inc(s_const, 1)
            nc.gpsimd.memset(tri_f, 1.0).then_inc(s_tri, 1)
            pool.wait_ge(s_const, 1)
            nc.gpsimd.affine_select(out=ident[:, :], in_=ident[:, :], compare_op=ALU.not_equal,
                                    fill=1.0, base=0, pattern=[[-1, P]], channel_multiplier=1
                                    ).then_inc(s_const, 1)
            pool.wait_ge(s_tri, 1)
            nc.gpsimd.affine_select(out=tri_f[:, 0:P], in_=tri_f[:, 0:P], compare_op=ALU.is_ge,
                                    fill=0.0, base=-1, pattern=[[1, P]], channel_multiplier=-1
                                    ).then_inc(s_tri, 1)

            def load_expert(e, par):
                pool.dma_start(stage[:, par, 0:HID],
                               w_gate[bass.ds(e, 1)].rearrange("a p n -> (a p) n")
                               ).then_inc(s_w[par], 16)
                pool.dma_start(stage[:, par, HID:2 * HID],
                               w_up[bass.ds(e, 1)].rearrange("a p n -> (a p) n")
                               ).then_inc(s_w[par], 16)
                pool.dma_start(stage[:, par, 2 * HID:3 * HID].rearrange("p (h c) -> p h c", c=D),
                               w_down[bass.ds(e, 1)].rearrange("a (h p) c -> (a p) h c", p=P)
                               ).then_inc(s_w[par], 16)

            def split_expert(e, par):
                pool.wait_ge(s_whi, 2 * (e + 1))
                hi = gu_w[:, bass.ds(e * 4 * HID, 2 * HID)].bitcast(F32)
                lo = gu_w[:, bass.ds(e * 4 * HID + 2 * HID, 2 * HID)]
                nc.gpsimd.tensor_tensor(out=lo, in0=stage[:, par, 0:2 * HID], in1=hi,
                                        op=ALU.subtract).then_inc(s_wlo, 1)
                hi = dn_w[:, bass.ds(e * 2 * HID, HID)].bitcast(F32)
                lo = dn_w[:, bass.ds(e * 2 * HID + HID, HID)]
                nc.gpsimd.tensor_tensor(out=lo, in0=stage[:, par, 2 * HID:3 * HID], in1=hi,
                                        op=ALU.subtract).then_inc(s_wlo, 1)

            load_expert(0, 0)
            load_expert(1, 1)
            with pool.Fori(0, E // 2 - 1) as it:
                for par in range(2):
                    split_expert(2 * it + par, par)
                    pool.wait_ge(s_wlo, 2 * (2 * it + par + 1))
                    load_expert(2 * it + par + 2, par)

            def scatter(g):
                pool.wait_ge(s_place, g + 1)
                pool.wait_ge(s_xnc, (g + 1) * NORM_STEPS // GROUPS)
                if g == 0:
                    pool.wait_ge(s_zeroed, 32)
                for b in range(g * BG, (g + 1) * BG):
                    for t in range(b * S, (b + 1) * S):
                        for k in range(TOPK):
                            pool.indirect_dma_start(
                                sorted_x[g], bass.IndirectOffsetOnAxis(ap=rows[:, k, t:t + 1], axis=0),
                                xn[:, t * D:(t + 1) * D], None).then_inc(s_sc[b % 2], 16)
                    if b > g * BG:
                        confirm(s_sc, s_scb, b - 1)
                confirm(s_sc, s_scb, (g + 1) * BG - 1)

            def confirm(landed, batches, b):
                pool.wait_ge(landed[b % 2], 16 * TOPK * S * (b // 2 + 1))
                pool.sem_inc(batches, 1)

            for par in range(2):
                split_expert(E - 2 + par, par)
            scatter(0)
            scatter(1)

            for b in range(B):
                if b % BG == 0:
                    for slot in range(2):
                        pool.wait_ge(s_yst[slot], 16 * (b // BG + 1) * NQ // 2)
                if b == 0:
                    pool.wait_ge(s_mw, 1)
                if b >= RING:
                    pool.wait_ge(s_fin, b - RING + 1)
                for j in range(S):
                    for k in range(TOPK):
                        t, slot = b * S + j, ((b % RING) * S + j) * TOPK + k
                        pool.indirect_dma_start(
                            ga[:, slot * D:(slot + 1) * D], None, sorted_y[b // BG],
                            bass.IndirectOffsetOnAxis(ap=rows[:, k, t:t + 1], axis=0)
                        ).then_inc(s_gt[b % 2], 16)
                if b >= 1:
                    confirm(s_gt, s_gtb, b - 1)
            confirm(s_gt, s_gtb, B - 1)

        @block.scalar
        def _(act):
            def norm_step(s, par, first, with_experts=False):
                act.wait_ge(s_var, s + 1)
                act.activation(std, var_eps, ACT.Sqrt).then_inc(s_std, 1)
                for n in range(2 if with_experts else 0):
                    act.wait_ge(s_w[n], 48 * (s + 1))
                    act.activation(gu_w[:, bass.ds((2 * s + n) * 4 * HID, 2 * HID)],
                                   stage[:, n, 0:2 * HID], ACT.Copy).then_inc(s_whi, 1)
                    act.activation(dn_w[:, bass.ds((2 * s + n) * 2 * HID, HID)],
                                   stage[:, n, 2 * HID:3 * HID], ACT.Copy).then_inc(s_whi, 1)
                act.wait_ge(s_xnr, s + 1)
                act.activation(xn[:, bass.ds(s * XW * D, XW * D)], x_in[par], ACT.Copy
                               ).then_inc(s_xnc, 1)
                for h in range(2):
                    act.wait_ge(s_xt, 2 * s + h + 1)
                    if not first:
                        act.wait_ge(s_lg, 2 * s + h - 1)
                    act.activation(xn_t[h], banks[h][:, :], ACT.Copy).then_inc(s_xte, 1)
                for h in range(2):
                    act.wait_ge(s_lg, 2 * s + h + 1)
                    act.activation(logits[:, bass.ds((2 * s + h) * S * E, S * E)],
                                   banks[2 + h][:, 0:S * E], ACT.Copy).then_inc(s_lge, 1)

            def route(g):
                act.wait_ge(s_gap, g + 1)
                for k, sign in enumerate((1.0, -1.0)):
                    act.activation(rw[:, k, g * SG:(g + 1) * SG], gap, ACT.Sigmoid, scale=sign
                                   ).then_inc(s_sig, 1)
                act.wait_ge(s_nv, g + 1)
                act.activation(max1, var_n[:, g * SG:(g + 1) * SG], ACT.Sqrt).then_inc(s_nsd, 1)

            norm_step(0, 0, True, True)
            norm_step(1, 1, False, True)
            with act.Fori(1, NORM_STEPS // 4) as it:
                for par in range(2):
                    norm_step(2 * it + par, par, False, True)
            assert NORM_STEPS // GROUPS * 2 == E
            route(0)
            with act.Fori(NORM_STEPS // 4, NORM_STEPS // 2) as it:
                for par in range(2):
                    norm_step(2 * it + par, par, False)
            route(1)
            act.wait_ge(s_params, 16 * 9)
            act.activation(decay_c, ld_c, ACT.Sigmoid).then_inc(s_dec, 1)

            def make_z(b, first):
                if first:
                    act.wait_ge(s_xnc, NORM_STEPS)
                    act.wait_ge(s_xt, 2 * NORM_STEPS)
                    act.wait_ge(s_mw, 1)
                else:
                    act.wait_ge(s_zt, b)
                for j in range(S):
                    last = act.activation(z[:, j * D:(j + 1) * D],
                                          xn[:, bass.ds((b * S + j) * D, D)], ACT.Copy,
                                          scale=var_n[:, bass.ds(b * S + j, 1)])
                last.then_inc(s_z, 1)
                act.wait_ge(s_zt, b + 1)
                if not first:
                    act.wait_ge(s_g, 2 * b)
                act.activation(zhl[:, 0, :], banks[0][:, :], ACT.Copy).then_inc(s_zh, 1)

            def v_out(b, c, first):
                act.wait_ge(s_v, 2 * b + c + 1)
                if not first:
                    act.wait_ge(s_yl, 2 * b + c - 1)
                act.activation(vpad[:, c, PAD:PAD + T], banks[1 + c][:, :], ACT.Identity,
                               bias=bias_c[:, CB + c:CB + c + 1]).then_inc(s_ve, 1)

            def tap_and_gate(b, first):
                for c in range(CB):
                    act.wait_ge(s_ve, 2 * b + c + 1)
                    if not first:
                        act.wait_ge(s_gvl, 2 * b + c - 1)
                    act.activation(acc[:, c * T:(c + 1) * T], vpad[:, c, 0:T], ACT.Identity,
                                   scale=dww_c[:, c * K:c * K + 1], bias=addb_c[:, c:c + 1]
                                   ).then_inc(s_t0, 1)
                if first:
                    act.wait_ge(s_wlo, 2 * E)
                for c in range(CB):
                    act.wait_ge(s_g, 2 * b + c + 1)
                    act.activation(gate[:, c, :], banks[3 + c][:, :], ACT.Sigmoid,
                                   bias=bias_c[:, c:c + 1]).then_inc(s_ge, 1)

            def mixer_a(b, first):
                make_z(b, first)
                for c in range(CB):
                    v_out(b, c, first)
                tap_and_gate(b, first)

            def mixer_b(b, more, with_final):
                if more:
                    make_z(b + 1, False)
                for c in range(CB):
                    act.wait_ge(s_y, 2 * b + c + 1)
                    if not (isinstance(b, int) and b == 0):
                        act.wait_ge(s_o, b)
                    act.activation(chl[:, 0, c, :], vpad[:, c, PAD:PAD + T], ACT.Copy
                                   ).then_inc(s_yh, 1)
                if more:
                    for c in range(CB):
                        v_out(b + 1, c, False)
                act.wait_ge(s_mx, 2 * b + 2)
                for c in range(CB):
                    act.wait_ge(s_gv, 2 * b + c + 1)
                    act.activation(chl[:, 0, c, :], acc[:, c * T:(c + 1) * T], ACT.Copy
                                   ).then_inc(s_gvh, 1)
                if with_final:
                    final(b - HEAD)
                if more:
                    tap_and_gate(b + 1, False)

            def final(b):
                act.wait_ge(s_fc, b + 1)
                v = ga[:, bass.ds((b % RING) * S * TOPK * D, S * TOPK * D)] \
                    .rearrange("p (j k d) -> p j k d", j=S, k=TOPK)[:, :, 0, :]
                act.activation(v, v, ACT.Silu).then_inc(s_fsi, 1)

            mixer_a(0, True)
            mixer_b(0, True, False)
            with act.Fori(1, HEAD - 1) as b:
                mixer_b(b, True, False)
            mixer_b(HEAD - 1, False, False)

            def expert_step(i, k, ends):
                nxt, prev, old = i + 1, i - 1, i - 2
                if not ends or nxt < TILES:
                    x_hi(nxt, (k + 1) % 2, ends)
                if not ends or i < TILES:
                    act.wait_ge(s_fg, i + 1)
                    if not ends or i >= 2:
                        act.wait_ge(s_ft, i - 1)
                    act.activation(silu_h[:, k % 2, :], banks[1 + k % 2][:, :], ACT.Silu
                                   ).then_inc(s_fs, 1)
                if not ends or 0 <= prev < TILES:
                    act.wait_ge(s_ft, prev + 1)
                    if not ends or prev >= 2:
                        act.wait_ge(s_fy, prev - 1)
                    act.activation(hhl[:, (k - 1) % 2, 0, :], banks[5 + (k - 1) % 2][:, :], ACT.Copy
                                   ).then_inc(s_fhh, 1)
                if not ends or 0 <= old < TILES:
                    slot, sub = ((k - 2) // QT) % 2, (k - 2) % QT
                    act.wait_ge(s_fy, old + 1)
                    if sub == 0 and (not ends or old >= 2 * QT):
                        act.wait_ge(s_yst[slot], 16 * (old // (2 * QT)) if ends
                                    else 2 * (old - 4 * slot))
                    act.activation(y_quad[:, slot, sub * D:(sub + 1) * D], banks[7][:, 0:D],
                                   ACT.Copy).then_inc(s_fye, 1)

            def x_hi(i, par, ends):
                act.wait_ge(s_fx, i + 1)
                if not ends or i >= 2:
                    act.wait_ge(s_fu, i - 1)
                act.activation(xhl[:, par, 0, :], banks[0][:, 0:P], ACT.Copy).then_inc(s_fxh, 1)

            act.wait_ge(s_gv, 2 * HEAD)
            x_hi(0, 0, True)
            experts_schedule(act.Fori, expert_step, 2)

            act.wait_ge(s_ft, TILES)
            make_z(HEAD, False)
            for c in range(CB):
                v_out(HEAD, c, False)
            tap_and_gate(HEAD, False)
            with act.Fori(HEAD, B - 1) as b:
                mixer_b(b, True, True)
            mixer_b(B - 1, False, True)
            with act.Fori(B - HEAD, B) as b:
                final(b)

        @block.vector
        def _(dve):
            V = nc.vector
            link = Linked(dve, s_dconst)
            link(V.memset(ones_f, 1.0))
            link(V.memset(minus1, -1.0))
            link(V.tensor_tensor_scan(out=ramp, data0=ones_f.to_broadcast([P, E]),
                                      data1=minus1.to_broadcast([P, E]), initial=float(E + 1),
                                      op0=ALU.mult, op1=ALU.add))
            dve.wait_ge(s_tri, 2)
            V.tensor_copy(tri, tri_f[:, 0:P]).then_inc(s_tri, 1)
            V.tensor_copy(ones_r, tri_f[:, P:2 * P]).then_inc(s_tri, 1)

            norm = Linked(dve, s_n)
            NORM_LINKS = 12

            def norm_step(s, par):
                norm.base, norm.n = s * NORM_LINKS, 0
                xs = x_in[par]
                dve.wait_ge(s_x[par], 32 * ((s - par) // 2 + 1) if isinstance(s, int)
                            else 16 * (s - par) + 32)
                for j in range(XW):
                    last = V.bn_stats(stats[:, j, :], xs[:, j * D:(j + 1) * D])
                norm(last)
                mean, var = meanvar[:, 0, :], meanvar[:, 1, :]
                V.tensor_tensor(out=mean, in0=stats[:, :, 1], in1=stats[:, :, 4], op=ALU.add)
                V.tensor_tensor(out=newton, in0=stats[:, :, 1], in1=stats[:, :, 4],
                                op=ALU.subtract)
                norm(V.tensor_tensor(out=var, in0=stats[:, :, 2], in1=stats[:, :, 5], op=ALU.add))
                V.tensor_scalar(out=mean, in0=mean, scalar1=0.5, scalar2=None, op0=ALU.mult)
                norm(V.tensor_tensor(out=newton, in0=newton, in1=newton, op=ALU.mult))
                norm(V.scalar_tensor_tensor(out=var, in0=newton, scalar=D / 4, in1=var,
                                            op0=ALU.mult, op1=ALU.add))
                norm(V.tensor_scalar(out=var, in0=var, scalar1=1.0 / D, scalar2=None,
                                     op0=ALU.mult))
                V.tensor_scalar(out=var_eps, in0=var, scalar1=EPS, scalar2=None,
                                op0=ALU.add).then_inc(s_var, 1)
                dve.wait_ge(s_std, s + 1)
                norm(V.reciprocal(rstd, std))
                norm(V.tensor_tensor(out=newton, in0=rstd, in1=rstd, op=ALU.mult))
                norm(V.tensor_tensor(out=newton, in0=newton, in1=var_eps, op=ALU.mult))
                norm(V.tensor_scalar(out=newton, in0=newton, scalar1=-0.5, scalar2=1.5,
                                     op0=ALU.mult, op1=ALU.add))
                norm(V.tensor_tensor(out=rstd, in0=rstd, in1=newton, op=ALU.mult))
                for j in range(XW):
                    last = V.tensor_scalar(out=xs[:, j * D:(j + 1) * D],
                                           in0=xs[:, j * D:(j + 1) * D],
                                           scalar1=mean[:, j:j + 1], scalar2=rstd[:, j:j + 1],
                                           op0=ALU.subtract, op1=ALU.mult)
                last.then_inc(s_xnr, 1)
                norm(V.tensor_tensor(out=newton, in0=rstd, in1=rstd, op=ALU.mult))
                norm(V.tensor_tensor(out=var_n[:, bass.ds(s * XW, XW)], in0=newton,
                                     in1=var, op=ALU.mult))
                assert norm.n == NORM_LINKS

            link = Linked(dve, s_r)

            def by_tile(a, n=E):
                return a.rearrange("p (t a) -> p t a", a=1).to_broadcast([P, SG, n])

            def pick(values, largest, marks):
                link(V.tensor_reduce(out=largest, in_=values, axis=AX.X, op=ALU.max))
                link(V.tensor_tensor(out=same, in0=values, in1=by_tile(largest), op=ALU.is_equal))
                link(V.tensor_tensor(out=same, in0=same,
                                     in1=ramp.rearrange("p (a e) -> p a e", a=1)
                                     .to_broadcast([P, SG, E]), op=ALU.mult))
                link(V.tensor_reduce(out=code_max, in_=same, axis=AX.X, op=ALU.max))
                link(V.tensor_tensor(out=marks, in0=same, in1=by_tile(code_max), op=ALU.is_equal))

            def route(g):
                lg = logits[:, g * GW:(g + 1) * GW].rearrange("p (t e) -> p t e", e=E)
                dve.wait_ge(s_lge, (g + 1) * BG)
                pick(lg, max1, first_e)
                link(V.scalar_tensor_tensor(out=rest, in0=first_e, scalar=-3e38, in1=lg,
                                            op0=ALU.mult, op1=ALU.add))
                pick(rest, max2, second_e)
                V.tensor_tensor(out=picked.rearrange("p (t e) -> p t e", e=E), in0=first_e,
                                in1=second_e, op=ALU.add).then_inc(s_pick, 1)
                V.tensor_tensor(out=gap, in0=max1, in1=max2, op=ALU.subtract).then_inc(s_gap, 1)
                link(V.tensor_scalar(out=var_n[:, g * SG:(g + 1) * SG],
                                     in0=var_n[:, g * SG:(g + 1) * SG], scalar1=EPS, scalar2=None,
                                     op0=ALU.add))
                dve.sem_inc(s_nv, 1)
                dve.wait_ge(s_cnt, g + 1)
                link(V.tensor_copy(per_tile, banks[4][:, 0:GW].rearrange("p (t e) -> p e t", e=E)))
                flat = [v.rearrange("p e t -> p (e t)") for v in (per_tile, running, before)]
                link(V.tensor_tensor_scan(out=flat[1], data0=ones_f.to_broadcast([P, GW]),
                                          data1=flat[0], initial=0.0, op0=ALU.mult, op1=ALU.add))
                link(V.tensor_tensor(out=flat[2], in0=flat[1], in1=flat[0], op=ALU.subtract))
                link(V.tensor_tensor(out=n_e, in0=running[:, :, SG - 1], in1=before[:, :, 0],
                                     op=ALU.subtract))
                link(V.tensor_scalar(out=ints[:, 0:E], in0=n_e, scalar1=float(P - 1), scalar2=None,
                                     op0=ALU.add))
                link(V.tensor_scalar(out=ints[:, 0:E], in0=ints[:, 0:E], scalar1=7, scalar2=None,
                                     op0=ALU.arith_shift_right))
                link(V.tensor_copy(tiles_e, ints[:, 0:E]))
                link(V.tensor_tensor_scan(out=ends_e, data0=ones_f.to_broadcast([P, E]),
                                          data1=tiles_e, initial=0.0, op0=ALU.mult, op1=ALU.add))
                link(V.tensor_tensor(out=base_e, in0=ends_e, in1=tiles_e, op=ALU.subtract))
                link(V.scalar_tensor_tensor(out=base_e, in0=base_e, scalar=float(P),
                                            in1=before[:, :, 0], op0=ALU.mult, op1=ALU.subtract))
                link(V.tensor_tensor(out=place, in0=before,
                                     in1=base_e.rearrange("p (e a) -> p e a", a=1)
                                     .to_broadcast([P, E, SG]), op=ALU.add))
                link(V.tensor_tensor(out=place, in0=place,
                                     in1=banks[5][:, 0:GW].rearrange("p (t e) -> p e t", e=E),
                                     op=ALU.add))
                for k, marks in enumerate((first_e, second_e)):
                    link(V.tensor_tensor(out=same, in0=marks,
                                         in1=place.rearrange("p e t -> p t e"), op=ALU.mult))
                    link(V.tensor_reduce(out=code_max, in_=same, axis=AX.X, op=ALU.add))
                    i0, i1, i2 = (ints[:, n * SG:(n + 1) * SG] for n in range(3))
                    link(V.tensor_copy(i0, code_max))
                    link(V.tensor_scalar(out=i1, in0=i0, scalar1=P - 1, scalar2=2,
                                         op0=ALU.bitwise_and, op1=ALU.logical_shift_left))
                    link(V.tensor_scalar(out=i2, in0=i0, scalar1=7, scalar2=QT - 1,
                                         op0=ALU.logical_shift_right, op1=ALU.bitwise_and))
                    link(V.tensor_scalar(out=i0, in0=i0, scalar1=9, scalar2=9,
                                         op0=ALU.logical_shift_right, op1=ALU.logical_shift_left))
                    link(V.tensor_tensor(out=i0, in0=i0, in1=i1, op=ALU.bitwise_or))
                    link(V.tensor_tensor(out=rows[:, k, g * SG:(g + 1) * SG], in0=i0.bitcast(U32),
                                         in1=i2.bitcast(U32), op=ALU.bitwise_or))
                dve.sem_inc(s_place, 1)
                link(V.tensor_tensor_scan(out=tile_no, data0=ones_f.to_broadcast([P, NT]),
                                          data1=ones_f.to_broadcast([P, NT]), initial=0.0,
                                          op0=ALU.mult, op1=ALU.add))
                link(V.tensor_tensor(out=past,
                                     in0=ends_e.rearrange("p (a e) -> p a e", a=1)
                                     .to_broadcast([P, NT, E]),
                                     in1=tile_no.rearrange("p (t a) -> p t a", a=1)
                                     .to_broadcast([P, NT, E]), op=ALU.is_lt))
                link(V.tensor_reduce(out=n_past, in_=past, axis=AX.X, op=ALU.add))
                link(V.tensor_scalar(out=tile_expert[:, g * NT:(g + 1) * NT], in0=n_past,
                                     scalar1=float(E - 1), scalar2=None, op0=ALU.min))
                dve.wait_ge(s_sig, 2 * (g + 1))
                both = rw[:, :, g * SG:(g + 1) * SG]
                link(V.tensor_scalar(out=both, in0=both, scalar1=DEPTH_SCALE, scalar2=None,
                                     op0=ALU.mult))
                dve.wait_ge(s_nsd, g + 1)
                v = var_n[:, g * SG:(g + 1) * SG]
                link(V.reciprocal(max2, max1))
                link(V.tensor_tensor(out=gap, in0=max2, in1=max2, op=ALU.mult))
                link(V.tensor_tensor(out=gap, in0=gap, in1=v, op=ALU.mult))
                link(V.tensor_scalar(out=gap, in0=gap, scalar1=-0.5, scalar2=1.5, op0=ALU.mult,
                                     op1=ALU.add))
                link(V.tensor_tensor(out=v, in0=max2, in1=gap, op=ALU.mult))

            half = NORM_STEPS // 4
            for g in range(GROUPS):
                with dve.Fori(g * half, (g + 1) * half) as it:
                    for par in range(2):
                        norm_step(2 * it + par, par)
                route(g)

            link = Linked(dve, s_prep)
            dve.wait_ge(s_params, 16 * 9)
            dve.wait_ge(s_mixraw, 16 * 3)
            dve.wait_ge(s_bmm, 1)
            link(V.tensor_tensor(out=bias_c, in0=inb_c, in1=banks[6][:, 0:4], op=ALU.add))
            link(V.tensor_tensor(out=addb_c, in0=dwb_c, in1=mixb_c, op=ALU.add))
            link(V.tensor_scalar(out=inw_raw, in0=inw_raw, scalar1=gamma_c, scalar2=None,
                                 op0=ALU.mult))
            for raw, w in ((inw_raw, inw[:, :, :]),
                           (mixw_raw, mixw[:, :, :, :].rearrange("p l c n -> p l (c n)")),
                           (outw_raw, outw[:, :, :, :].rearrange("p l c n -> p l (c n)")),
                           (outb_f[:, :], outb[:, 0:2, :])):
                link(V.tensor_copy(w[:, 0], raw))
                link(V.tensor_tensor(out=w[:, 1], in0=raw, in1=w[:, 0].bitcast(F32),
                                     op=ALU.subtract))
            link(V.tensor_copy(outb[:, 2, :], ones_f[0:1, :].to_broadcast([1, D])))
            dve.wait_ge(s_lg, 2 * NORM_STEPS)
            link(V.memset(vpad[:, :, 0:PAD], 0.0))
            dve.sem_inc(s_mw, 1)

            steps = Linked(dve, s_c)
            MIXER_LINKS = CB * (K - 1) + 2 * CB

            def z_lo(b, first):
                dve.wait_ge(s_zh, b + 1)
                if not first:
                    dve.wait_ge(s_g, 2 * b)
                V.tensor_tensor(out=zhl[:, 1, :], in0=banks[0][:, :], in1=zhl[:, 0, :].bitcast(F32),
                                op=ALU.subtract).then_inc(s_zl, 1)

            def conv(b, c):
                dve.wait_ge(s_t0, 2 * b + c + 1)
                a = acc[:, c * T:(c + 1) * T]
                for k in range(1, K):
                    steps(V.scalar_tensor_tensor(out=a, in0=vpad[:, c, k:k + T],
                                                 scalar=dww_c[:, c * K + k:c * K + k + 1], in1=a,
                                                 op0=ALU.mult, op1=ALU.add))

            def scan(b, c):
                v = vpad[:, c, PAD:PAD + T]
                V.tensor_tensor_scan(out=v, data0=decay_c[:, c:c + 1].to_broadcast([P, T]),
                                     data1=v, initial=0.0, op0=ALU.mult, op1=ALU.add
                                     ).then_inc(s_y, 1)

            def split(b, c, src, ready, done):
                dve.wait_ge(ready, 2 * b + c + 1)
                V.tensor_tensor(out=chl[:, 1, c, :], in0=src, in1=chl[:, 0, c, :].bitcast(F32),
                                op=ALU.subtract).then_inc(done, 1)

            def s_out(b):
                dve.wait_ge(s_o, b + 1)
                dve.wait_ge(s_scb, b + 1)
                v = xn[:, bass.ds(b * S * D, S * D)]
                V.tensor_tensor(out=v, in0=v, in1=banks[7][:, :], op=ALU.add).then_inc(s_s, 1)

            def mixer_b(b, more, with_final):
                steps.base, steps.n = b * MIXER_LINKS, 0
                conv(b, 0)
                if more:
                    z_lo(b + 1, False)
                scan(b, 0)
                conv(b, 1)
                split(b, 0, vpad[:, 0, PAD:PAD + T], s_yh, s_yl)
                scan(b, 1)
                if with_final:
                    combine(b - HEAD)
                split(b, 1, vpad[:, 1, PAD:PAD + T], s_yh, s_yl)
                for c in range(CB):
                    a = acc[:, c * T:(c + 1) * T]
                    dve.wait_ge(s_mx, 2 * b + c + 1)
                    steps(V.tensor_tensor(out=a, in0=a, in1=banks[5 + c][:, :], op=ALU.add))
                    dve.wait_ge(s_ge, 2 * b + c + 1)
                    steps(V.tensor_tensor(out=a, in0=a, in1=gate[:, c, :], op=ALU.mult))
                    dve.sem_inc(s_gv, 1)
                for c in range(CB):
                    split(b, c, acc[:, c * T:(c + 1) * T], s_gvh, s_gvl)
                assert steps.n == MIXER_LINKS
                if with_final:
                    finish(b - HEAD)
                s_out(b)

            combine_steps = Linked(dve, s_f)

            def combine(b):
                combine_steps.base, combine_steps.n = b * 2, 0
                dve.wait_ge(s_gtb, b + 1)
                v = ga[:, bass.ds((b % RING) * S * TOPK * D, S * TOPK * D)] \
                    .rearrange("p (j k d) -> p j k d", j=S, k=TOPK)
                for j in range(S):
                    last = V.tensor_scalar(out=v[:, j, 0, :], in0=v[:, j, 0, :],
                                           scalar1=rw[:, 0, bass.ds(b * S + j, 1)], scalar2=None,
                                           op0=ALU.mult)
                combine_steps(last)
                for j in range(S):
                    last = V.scalar_tensor_tensor(out=v[:, j, 0, :], in0=v[:, j, 1, :],
                                                  scalar=rw[:, 1, bass.ds(b * S + j, 1)],
                                                  in1=v[:, j, 0, :], op0=ALU.mult, op1=ALU.add)
                last.then_inc(s_fc, 1)

            def finish(b):
                combine_steps.base, combine_steps.n = b * 2 + 1, 0
                dve.wait_ge(s_fsi, b + 1)
                dve.wait_ge(s_s, b + 1)
                v = ga[:, bass.ds((b % RING) * S * TOPK * D, S * TOPK * D)] \
                    .rearrange("p (j k d) -> p j k d", j=S, k=TOPK)[:, :, 0, :]
                s_b = xn[:, bass.ds(b * S * D, S * D)].rearrange("p (j d) -> p j d", d=D)
                combine_steps(V.tensor_tensor(out=v, in0=v, in1=s_b, op=ALU.mult))
                dve.wait_ge(s_xb, 16 * (b + 1))
                xb = x_back.rearrange("p (j d) -> p j d", d=D)
                V.tensor_tensor(out=xb, in0=xb, in1=v, op=ALU.add).then_inc(s_fin, 1)

            dve.wait_ge(s_dec, 1)
            z_lo(0, True)
            mixer_b(0, True, False)
            with dve.Fori(1, HEAD - 1) as b:
                mixer_b(b, True, False)
            mixer_b(HEAD - 1, False, False)

            def x_lo(i, par):
                dve.wait_ge(s_fxh, i + 1)
                V.tensor_tensor(out=xhl[:, par, 1, :], in0=banks[0][:, 0:P],
                                in1=xhl[:, par, 0, :].bitcast(F32), op=ALU.subtract
                                ).then_inc(s_fxl, 1)

            def expert_step(i, k, ends):
                if not ends or i + 1 < TILES:
                    x_lo(i + 1, (k + 1) % 2)
                if not ends or i < TILES:
                    h = silu_h[:, k % 2, :]
                    dve.wait_ge(s_fs, i + 1)
                    dve.wait_ge(s_fu, i + 1)
                    V.tensor_tensor(out=h, in0=h, in1=banks[3 + k % 2][:, :], op=ALU.mult
                                    ).then_inc(s_fh, 1)
                if not ends or 0 <= i - 1 < TILES:
                    par = (k - 1) % 2
                    dve.wait_ge(s_fhh, i)
                    V.tensor_tensor(out=hhl[:, par, 1, :], in0=banks[5 + par][:, :],
                                    in1=hhl[:, par, 0, :].bitcast(F32), op=ALU.subtract
                                    ).then_inc(s_fhl, 1)

            x_lo(0, 0)
            experts_schedule(dve.Fori, expert_step, 2)

            z_lo(HEAD, False)
            with dve.Fori(HEAD, B - 1) as b:
                mixer_b(b, True, True)
            mixer_b(B - 1, False, True)
            with dve.Fori(B - HEAD, B) as b:
                combine(b)
                finish(b)

        @block.tensor
        def _(pe):
            mm = nc.tensor.matmul

            def three(out_ps, stat, mov, start, stop):
                mm(out_ps, stat[0], mov[0], start=start, stop=False)
                mm(out_ps, stat[0], mov[1], start=False, stop=False)
                return mm(out_ps, stat[1], mov[0], start=False, stop=stop)

            def norm_step(s, par, first):
                pe.wait_ge(s_xnr, s + 1)
                for h in range(2):
                    if not first:
                        pe.wait_ge(s_xte, 2 * s + h - 1)
                    for j in range(S):
                        t = h * S + j
                        last = nc.tensor.transpose(banks[h][:, j * P:(j + 1) * P],
                                                   x_in[par][:, t * D:(t + 1) * D], ident[:, :])
                    last.then_inc(s_xt, 1)
                for h in range(2):
                    pe.wait_ge(s_xte, 2 * s + h + 1)
                    if not first:
                        pe.wait_ge(s_lge, 2 * s + h - 1)
                    for j in range(S):
                        last = mm(banks[2 + h][:, j * E:(j + 1) * E], xn_t[h][:, j * P:(j + 1) * P],
                                  route_w[:, :], start=True, stop=True)
                    last.then_inc(s_lg, 1)

            def count(g):
                pe.wait_ge(s_pick, g + 1)
                if g:
                    pe.wait_ge(s_place, g)
                mm(banks[4][:, 0:GW], ones_r, picked, start=True, stop=True)
                mm(banks[5][:, 0:GW], tri, picked, start=True, stop=True).then_inc(s_cnt, 1)

            pe.wait_ge(s_const, 2)
            pe.wait_ge(s_params, 16 * 9)
            pe.wait_ge(s_tri, 4)
            norm_step(0, 0, True)
            norm_step(1, 1, False)
            with pe.Fori(1, NORM_STEPS // 4) as it:
                for par in range(2):
                    norm_step(2 * it + par, par, False)
            count(0)
            with pe.Fori(NORM_STEPS // 4, NORM_STEPS // 2) as it:
                for par in range(2):
                    norm_step(2 * it + par, par, False)
            count(1)
            pe.wait_ge(s_mixraw, 48)
            for n in range(2 * CB):
                last = mm(banks[6][:, n:n + 1], inw_raw[:, n * P:(n + 1) * P], beta_c,
                          start=True, stop=True)
            last.then_inc(s_bmm, 1)

            def z_turn(b, first):
                pe.wait_ge(s_z, b + 1)
                if first:
                    pe.wait_ge(s_mw, 1)
                else:
                    pe.wait_ge(s_zl, b)
                for j in range(S):
                    last = nc.tensor.transpose(banks[0][:, j * P:(j + 1) * P],
                                               z[:, j * D:(j + 1) * D], ident[:, :])
                last.then_inc(s_zt, 1)

            def project(b, first):
                pe.wait_ge(s_zl, b + 1)
                for kind, done, emptied, bank in ((1, s_v, s_ve, 1), (0, s_g, s_ge, 3)):
                    for c in range(CB):
                        if not first:
                            pe.wait_ge(emptied, 2 * b + c - 1)
                        n = (kind * CB + c) * P
                        three(banks[bank + c][:, :], [inw[:, l, n:n + P] for l in range(2)],
                              [zhl[:, l, :] for l in range(2)], True, True).then_inc(done, 1)

            def mixer_b(b, more, with_final):
                if more:
                    z_turn(b + 1, False)
                    project(b + 1, False)
                pe.wait_ge(s_yl, 2 * b + 2)
                for m in range(CB):
                    for c in range(CB):
                        last = three(banks[5 + m][:, :],
                                     [mixw[:, l, c, m * P:(m + 1) * P] for l in range(2)],
                                     [chl[:, l, c, :] for l in range(2)], c == 0, c == CB - 1)
                    last.then_inc(s_mx, 1)
                if not (isinstance(b, int) and b == 0):
                    pe.wait_ge(s_s, b)
                pe.wait_ge(s_gvl, 2 * b + 2)
                for j in range(S):
                    o = banks[7][:, j * D:(j + 1) * D]
                    mm(o, outb[0:1, 2, :], outb[0:1, 0, :], start=True, stop=False)
                    mm(o, outb[0:1, 2, :], outb[0:1, 1, :], start=False, stop=False)
                    for c in range(CB):
                        last = three(o, [chl[:, l, c, j * P:(j + 1) * P] for l in range(2)],
                                     [outw[:, l, c, :] for l in range(2)], False, c == CB - 1)
                last.then_inc(s_o, 1)

            z_turn(0, True)
            project(0, True)
            mixer_b(0, True, False)
            with pe.Fori(1, HEAD - 1) as b:
                mixer_b(b, True, False)
            mixer_b(HEAD - 1, False, False)

            def x_turn(i, k, ends):
                slot, sub = (k // QT) % 2, k % QT
                if sub == 0:
                    pe.wait_ge(s_q[slot], 16 * (i // (2 * QT) + 1) if ends
                               else 2 * (i - 4 * slot) + 16)
                if not ends or i >= 1:
                    pe.wait_ge(s_fxl, i)
                nc.tensor.transpose(banks[0][:, 0:P], x_quad[:, slot, sub * P:(sub + 1) * P],
                                    ident[:, :]).then_inc(s_fx, 1)

            def expert_step(i, k, ends):
                if k == 0:
                    experts.clear()
                    for n in range(-2 if not ends or i >= 2 else 0, 8 if not ends or i < TILES else 0):
                        experts[n] = pe.value_load(tile_expert[0:1, bass.ds(i + n, 1)],
                                                   min_val=0, max_val=E - 1)
                if not ends or i + 1 < TILES:
                    x_turn(i + 1, (k + 1) % 8, ends)
                if not ends or i < TILES:
                    w = experts[k] * (4 * HID)
                    pe.wait_ge(s_fxl, i + 1)
                    for half, done, emptied in ((0, s_fg, s_fs), (1, s_fu, s_fh)):
                        if not ends or i >= 2:
                            pe.wait_ge(emptied, i - 1)
                        three(banks[1 + 2 * half + k % 2][:, :],
                              [xhl[:, k % 2, l, :] for l in range(2)],
                              [gu_w[:, bass.ds(w + l * 2 * HID + half * HID, HID)]
                               for l in range(2)], True, True).then_inc(done, 1)
                if not ends or 0 <= i - 1 < TILES:
                    par = (k - 1) % 2
                    pe.wait_ge(s_fh, i)
                    if not ends or i - 1 >= 2:
                        pe.wait_ge(s_fhl, i - 2)
                    for n in range(HB):
                        last = nc.tensor.transpose(banks[5 + par][:, n * P:(n + 1) * P],
                                                   silu_h[:, par, n * P:(n + 1) * P], ident[:, :])
                    last.then_inc(s_ft, 1)
                if not ends or 0 <= i - 2 < TILES:
                    par = k % 2
                    w = experts[k - 2] * (2 * HID)
                    pe.wait_ge(s_fhl, i - 1)
                    if not ends or i - 2 >= 1:
                        pe.wait_ge(s_fye, i - 2)
                    for n in range(HB):
                        last = three(banks[7][:, 0:D],
                                     [hhl[:, par, l, n * P:(n + 1) * P] for l in range(2)],
                                     [dn_w[:, bass.ds(w + l * HID + n * D, D)] for l in range(2)],
                                     n == 0, n == HB - 1)
                    last.then_inc(s_fy, 1)

            experts = {}
            pe.wait_ge(s_wlo, 2 * E)
            pe.wait_ge(s_s, HEAD)
            x_turn(0, 0, True)
            experts_schedule(pe.Fori, expert_step, 2)

            pe.wait_ge(s_fye, TILES)
            z_turn(HEAD, False)
            project(HEAD, False)
            with pe.Fori(HEAD, B - 1) as b:
                mixer_b(b, True, True)
            mixer_b(B - 1, False, True)


_INS = ['L0_attn_x', 'L0_attn_norm_gamma', 'L0_attn_norm_beta', 'L0_attn_in_w', 'L0_attn_in_b',
        'L0_attn_dw_w', 'L0_attn_dw_b', 'L0_attn_log_decay', 'L0_attn_mix_w', 'L0_attn_mix_b',
        'L0_attn_out_w', 'L0_attn_out_b', 'L0_ffn_Wr', 'L0_ffn_Wg', 'L0_ffn_Wu', 'L0_ffn_Wd']


def kernel(**inputs):
    import numpy as _np
    import concourse.bacc as _bacc
    from concourse import mybir as _mybir
    from concourse.bass_utils import run_bass_kernel_spmd as _run

    nc = _bacc.Bacc("TRN2", target_bir_lowering=False, num_devices=1)
    arrays, args = {}, []
    for name in _INS:
        a = _np.ascontiguousarray(inputs[name])
        arrays[f"in_{name}_dram"] = a
        args.append(nc.dram_tensor(f"in_{name}_dram", a.shape, _mybir.dt.from_np(a.dtype),
                                   kind="ExternalInput").ap())
    shape = arrays["in_L0_attn_x_dram"].shape
    args.append(nc.dram_tensor("out_dram", shape, _mybir.dt.float32, kind="ExternalOutput").ap())
    recurrent_moe_block(nc, *args)
    r = _run(nc, [arrays], core_ids=[0])
    return r.results[0]["out_dram"]
```

```python
import concourse.bass as bass
from concourse import mybir
from contextlib import ExitStack


def recurrent_moe_block(nc, x, gamma, beta, in_w, in_b, dw_w, dw_b, log_decay, mix_w, mix_b,
                        out_w, out_b, w_route, w_gate, w_up, w_down, out):
    F32, F32R, I32, U32 = mybir.dt.float32, mybir.dt.float32r, mybir.dt.int32, mybir.dt.uint32
    ALU, ACT, AX = mybir.AluOpType, mybir.ActivationFunctionType, mybir.AxisListType

    P = 128
    B, T, D = x.shape
    H = in_w.shape[1] // 2
    K = dw_w.shape[1]
    E, _, HID = w_gate.shape
    TOPK = 2
    PAD = K - 1
    CB = H // P
    HB = HID // P
    S = T // P
    NS = B * S
    GROUPS = 2
    BG, SG = B // GROUPS, NS // GROUPS
    QT = 4
    NT = -(-(SG * TOPK + E - 1) // 8) * 8
    NQ = NT // QT
    TILES = GROUPS * NT
    EPS = 1e-5
    DEPTH_SCALE = 1.0 / (12 ** 0.5)
    ITERS = TILES // 8
    HEAD = 2
    MIX_LAST = B - HEAD
    FIN_FIRST = MIX_LAST - 2
    FIN_IN = ITERS - FIN_FIRST
    RING = 3

    x_v = x.rearrange("b (j p) d -> b p j d", p=P)
    out_v = out.rearrange("b (j p) d -> b p j d", p=P)
    sorted_x = [nc.dram_tensor(f"sorted_x{g}", [NT * P, D], F32, kind="Internal").ap()
                for g in range(GROUPS)]
    sorted_y = [nc.dram_tensor(f"sorted_y{g}", [NT * P, D], F32, kind="Internal").ap()
                for g in range(GROUPS)]
    sx_v = [v.rearrange("(q p s) d -> q p (s d)", p=P, s=QT) for v in sorted_x]
    sy_v = [v.rearrange("(q p s) d -> q p (s d)", p=P, s=QT) for v in sorted_y]

    ctx = ExitStack()
    with ctx:
        def sb(name, shape, dt=F32):
            return ctx.enter_context(nc.sbuf_tensor(name, shape, dt))

        def sem(name):
            return ctx.enter_context(nc.semaphore(name))

        xn = sb("xn", [P, NS * D])
        gu_w = sb("gu_w", [P, E * 2 * 2 * HID], F32R)
        dn_w = sb("dn_w", [P, E * 2 * HB * D], F32R)
        inw = sb("inw", [P, 2, 2 * H], F32R)
        mixw = sb("mixw", [P, 2, CB, H], F32R)
        outw = sb("outw", [P, 2, CB, D], F32R)
        ident = sb("ident", [P, P])
        route_w = sb("route_w", [P, E])
        rows = sb("rows", [P, TOPK, NS], U32)
        rw = sb("rw", [P, TOPK, NS])
        tile_expert = sb("tile_expert", [P, TILES], I32)
        var_n = sb("var_n", [P, NS])
        params = sb("params", [P, 64])
        gamma_c, beta_c = params[:, 0:1], params[:, 1:2]
        inb_c, bias_c = params[:, 2:6], params[:, 6:10]
        dww_c = params[:, 10:10 + CB * K]
        dwb_c, mixb_c, addb_c = params[:, 24:26], params[:, 26:28], params[:, 28:30]
        ld_c, decay_c = params[:, 30:32], params[:, 32:34]
        ramp = params[:, 34:42]
        outb_c = params[:, 44:45]
        ones_f = params[:, 42:43]
        minus1 = params[:, 43:44]
        work = sb("work", [P, 6 * HID])
        stage = work[:, :].rearrange("p (r n) -> p r n", r=2)
        silu_h = work[:, 0:2 * HID].rearrange("p (r n) -> p r n", r=2)
        x_quad = work[:, 2 * HID:4 * HID].rearrange("p (r n) -> p r n", r=2)
        y_quad = work[:, 4 * HID:6 * HID].rearrange("p (r n) -> p r n", r=2)
        xhl = sb("xhl", [P, 2, 2, P], F32R)
        hhl = sb("hhl", [P, 2, 2, HID], F32R)
        zhl = sb("zhl", [P, 2, T], F32R)
        vpad = sb("vpad", [P, CB, PAD + T])
        acc = sb("acc", [P, CB * T])
        chl = sb("chl", [P, 2, CB, T], F32R)
        gates = sb("gates", [P, CB * T])
        gate = gates[:, :].rearrange("p (c t) -> p c t", c=CB)
        logits, inw_raw = gates[:, 0:NS * E], gates[:, NS * E:NS * E + 2 * H]
        mixed_t = sb("mixed_t", [P, T])
        xr = sb("xr", [P, 2 * T])
        x_back = xr[:, 0:T]
        z = xr[:, T:2 * T]
        x_in = [xr[:, :], acc[:, :]]
        xn_t = [vpad[:, 0, 0:T], vpad[:, 1, 0:T]]
        tri = zhl[:, 0, 0:P]
        ones_r = zhl[:, 0, P:2 * P]
        picked = chl[:, 0, 0, 0:SG * E]
        ga = sb("ga", [P, RING * S * TOPK * D])
        at = [0]

        def scratch(*shape):
            n = 1
            for s in shape:
                n *= s
            v = ga[:, at[0]:at[0] + n]
            at[0] += n
            assert at[0] <= RING * S * TOPK * D
            return v if len(shape) == 1 else v.rearrange("p (a b) -> p a b", a=shape[0])

        mixw_raw, outw_raw = scratch(CB * H), scratch(CB * D)
        tri_f = scratch(2 * P)
        same = scratch(SG, E)
        marks_at = at[0]
        first_e, second_e, rest = (scratch(SG, E) for _ in range(3))
        max1, max2, code_max, gap = (scratch(SG) for _ in range(4))
        running, before = (scratch(E, SG) for _ in range(2))
        per_tile = rest.rearrange("p t e -> p (t e)").rearrange("p (e t) -> p e t", e=E)
        place = running
        n_e, tiles_e, ends_e, base_e = (scratch(E) for _ in range(4))
        tile_no = scratch(NT)
        past = ga[:, marks_at:marks_at + NT * E].rearrange("p (a b) -> p a b", a=NT)
        assert NT * E <= 3 * SG * E
        n_past = tile_no
        small = sb("small", [P, 2 * S * 8 + 6 * 2 * S])
        stats = small[:, 0:48].rearrange("p (j k) -> p j k", k=6)
        meanvar = small[:, 48:64].rearrange("p (k j) -> p k j", k=2)
        var_eps, std, rstd, newton = (small[:, 64 + 8 * k:72 + 8 * k] for k in range(4))
        ints = sb("ints", [P, 4 * SG], I32)

        XT, GP, UP, HT, YP, MA, MB, MC = range(8)
        banks = [ctx.enter_context(nc.psum_tensor(f"bank{k}", [P, 512], F32)) for k in range(8)]

        s_params = sem("params_loaded")
        s_mixraw = sem("mixer_weights_loaded")
        s_x = [sem("x_loaded_0"), sem("x_loaded_1")]
        s_const = sem("constants_built")
        s_tri = sem("triangle_built")
        s_dconst = sem("vector_constants")
        s_zero = sem("zeros_built")
        s_zeroed = [sem(f"sorted_x{g}_zeroed") for g in range(GROUPS)]
        s_w = [sem("expert_loaded_0"), sem("expert_loaded_1")]
        s_whi = sem("expert_hi")
        s_wlo = sem("expert_lo")
        s_n = sem("norm_steps")
        s_var = sem("variance_ready")
        s_std = sem("std_ready")
        s_xnr = sem("xn_ready")
        s_xnc = sem("xn_kept")
        s_xt = sem("xn_transposed")
        s_xte = sem("xn_t_ready")
        s_lg = sem("logits_summed")
        s_lge = sem("logits_ready")
        s_r = sem("route_steps")
        s_pick = sem("experts_picked")
        s_cnt = sem("pairs_counted")
        s_gap = sem("logit_gap")
        s_sig = sem("expert_weights")
        s_nv = sem("xn_variance_eps")
        s_nsd = sem("xn_std")
        s_place = sem("places_ready")
        s_sc = [sem("scatter_even"), sem("scatter_odd")]
        s_scb = sem("batches_scattered")
        s_prep = sem("prep_steps")
        s_bmm = sem("bias_product")
        s_dec = sem("decay_ready")
        s_mw = sem("mixer_weights_ready")
        s_q = [sem("x_quad_loaded_0"), sem("x_quad_loaded_1")]
        s_fx = sem("tile_transposed")
        s_fxh = sem("tile_hi")
        s_fxl = sem("tile_lo")
        s_fg = sem("gate_product")
        s_fu = sem("up_product")
        s_fs = sem("silu_ready")
        s_fh = sem("hidden_ready")
        s_ft = sem("hidden_transposed")
        s_fhh = sem("hidden_hi")
        s_fhl = sem("hidden_lo")
        s_fy = sem("down_product")
        s_fyh = sem("y_half")
        s_fye = sem("y_ready")
        s_yst = [sem("y_quad_stored_0"), sem("y_quad_stored_1")]
        s_z = sem("z_ready")
        s_zt = sem("z_transposed")
        s_zh = sem("z_hi")
        s_zl = sem("z_lo")
        s_v = sem("v_product")
        s_g = sem("g_product")
        s_ve = sem("v_ready")
        s_ge = sem("gate_ready")
        s_t0 = sem("first_tap")
        s_c = sem("mixer_steps")
        s_y = sem("state_ready")
        s_yh = sem("state_hi")
        s_yl = sem("state_lo")
        s_mx = sem("mix_product")
        s_gv = sem("gated_sum")
        s_gvh = sem("gated_hi")
        s_gvl = sem("gated_lo")
        s_o = sem("out_product")
        s_oe = sem("out_copied")
        s_ot = sem("out_transposed")
        s_s = sem("s_ready")
        s_gt = [sem("gather_even"), sem("gather_odd")]
        s_gtb = sem("batches_gathered")
        s_xb = sem("x_back_loaded")
        s_f = sem("combine_steps")
        s_fc = sem("ffn_combined")
        s_fsi = sem("ffn_silu")
        s_fin = sem("result_ready")
        s_out = sem("result_stored")

        block = ctx.enter_context(nc.Block())

        class Linked:

            def __init__(self, engine, counter):
                self.engine, self.counter, self.base, self.n = engine, counter, 0, 0

            def __call__(self, instruction, wait=True):
                self.n += 1
                instruction.then_inc(self.counter, 1)
                if wait:
                    self.engine.wait_ge(self.counter, self.base + self.n)

        def down_part(e, half):
            return dn_w[:, bass.ds(e * 2 * HID, 2 * HID)] \
                .rearrange("p (h l c) -> p h l c", h=HB, l=2)[:, :, half, :]

        XW = 2 * S
        NORM_STEPS = B // 2
        GW = SG * E

        def experts_schedule(fori, step):
            def iteration(it, ends, mix, fin):
                for k in range(8):
                    step(it * 8 + k, k, ends, mix, fin)

            iteration(0, True, None, None)
            with fori(1, FIN_FIRST) as it:
                iteration(it, False, it + HEAD - 1, None)
            with fori(FIN_FIRST, MIX_LAST) as it:
                iteration(it, False, it + HEAD - 1, it - FIN_FIRST)
            iteration(MIX_LAST, True, B - 1, MIX_LAST - FIN_FIRST)
            with fori(MIX_LAST + 1, ITERS - 1) as it:
                iteration(it, False, None, it - FIN_FIRST)
            iteration(ITERS - 1, True, None, FIN_IN - 1)
            for k in range(2):
                step(TILES + k, k, True, None, None)

        def more(b):
            return not isinstance(b, int) or b + 1 < B

        def past_first(b):
            return not isinstance(b, int) or b > 0

        @block.sync
        def _(sp):
            def load_x(step_, par):
                for h in range(2):
                    sp.dma_start(x_in[par].rearrange("p (h j d) -> p h j d", h=2, d=D)[:, h],
                                 x_v[bass.ds(2 * step_ + h, 1)].rearrange("a p j d -> (a p) j d")
                                 ).then_inc(s_x[par], 16)

            def zero_list(g):
                zeros = hhl[:, 0, 0, :].bitcast(F32).rearrange("p (a n) -> p a n", a=1)
                sp.dma_start(sx_v[g].rearrange("q p n -> p q n"),
                             zeros.to_broadcast([P, NQ, HID])).then_inc(s_zeroed[g], 16)

            load_x(0, 0)
            for dst, src in ((route_w[:, :], w_route),
                             (gamma_c, gamma.rearrange("(p a) -> p a", a=1)),
                             (beta_c, beta.rearrange("(p a) -> p a", a=1)),
                             (inb_c, in_b.rearrange("(c p) -> p c", p=P)),
                             (dww_c.rearrange("p (c k) -> p c k", c=CB),
                              dw_w.rearrange("(c p) k -> p c k", p=P)),
                             (dwb_c, dw_b.rearrange("(c p) -> p c", p=P)),
                             (mixb_c, mix_b.rearrange("(c p) -> p c", p=P)),
                             (ld_c, log_decay.rearrange("(c p) -> p c", p=P)),
                             (outb_c, out_b.rearrange("(p a) -> p a", a=1))):
                with nc.allow_non_contiguous_dma(reason="a few small parameters"):
                    sp.dma_start(dst, src).then_inc(s_params, 16)
            sp.dma_start(inw_raw, in_w).then_inc(s_mixraw, 16)
            sp.dma_start(mixw_raw.rearrange("p (c n) -> p c n", c=CB),
                         mix_w.rearrange("(c p) n -> p c n", p=P)).then_inc(s_mixraw, 16)
            sp.dma_start(outw_raw.rearrange("p (c n) -> p c n", c=CB),
                         out_w.rearrange("(c p) n -> p c n", p=P)).then_inc(s_mixraw, 16)
            load_x(1, 1)
            sp.wait_ge(s_zero, 1)
            zero_list(0)
            with sp.Fori(1, NORM_STEPS // 2) as it:
                for par in range(2):
                    transposed = sp.snap(4 * it + 2 * par - 2)
                    sp.wait_ge(s_xnc, 2 * it + par - 1)
                    sp.wait_ge(s_xt, transposed)
                    load_x(2 * it + par, par)
            zero_list(1)

            def quad_in(g, q, slot, reuse):
                if reuse:
                    sp.wait_ge(s_fx, (g * NQ + q - 1) * QT)
                sp.dma_start(x_quad[:, slot, :],
                             sx_v[g][bass.ds(q, 1)].rearrange("a p n -> (a p) n")
                             ).then_inc(s_q[slot], 16)

            def quad_out(g, q, slot):
                sp.wait_ge(s_fye, (g * NQ + q + 1) * QT)
                sp.dma_start(sy_v[g][bass.ds(q, 1)].rearrange("a p n -> (a p) n"),
                             y_quad[:, slot, :]).then_inc(s_yst[slot], 16)

            sp.wait_ge(s_wlo, 2 * E)
            for g in range(GROUPS):
                sp.wait_ge(s_scb, (g + 1) * BG)
                for slot in range(2):
                    quad_in(g, slot, slot, g > 0)
                    if g:
                        quad_out(g - 1, NQ - 2 + slot, slot)
                with sp.Fori(1, NQ // 2) as it:
                    for slot in range(2):
                        quad_in(g, 2 * it + slot, slot, True)
                        quad_out(g, 2 * it + slot - 2, slot)
            for slot in range(2):
                quad_out(GROUPS - 1, NQ - 2 + slot, slot)
            for slot in range(2):
                sp.wait_ge(s_yst[slot], 16 * GROUPS * NQ // 2)

        @block.gpsimd
        def _(pool):
            nc.gpsimd.memset(hhl[:, 0, 0, :].bitcast(F32), 0.0
                             ).then_inc(s_zero, 1)
            nc.gpsimd.memset(ident[:, :], 0.0).then_inc(s_const, 1)
            nc.gpsimd.memset(tri_f, 1.0).then_inc(s_tri, 1)
            pool.wait_ge(s_const, 1)
            nc.gpsimd.affine_select(out=ident[:, :], in_=ident[:, :], compare_op=ALU.not_equal,
                                    fill=1.0, base=0, pattern=[[-1, P]], channel_multiplier=1
                                    ).then_inc(s_const, 1)
            pool.wait_ge(s_tri, 1)
            nc.gpsimd.affine_select(out=tri_f[:, 0:P], in_=tri_f[:, 0:P], compare_op=ALU.is_ge,
                                    fill=0.0, base=-1, pattern=[[1, P]], channel_multiplier=-1
                                    ).then_inc(s_tri, 1)

            def load_expert(e, par):
                pool.dma_start(stage[:, par, 0:HID],
                               w_gate[bass.ds(e, 1)].rearrange("a p n -> (a p) n")
                               ).then_inc(s_w[par], 16)
                pool.dma_start(stage[:, par, HID:2 * HID],
                               w_up[bass.ds(e, 1)].rearrange("a p n -> (a p) n")
                               ).then_inc(s_w[par], 16)
                pool.dma_start(stage[:, par, 2 * HID:3 * HID].rearrange("p (h c) -> p h c", c=D),
                               w_down[bass.ds(e, 1)].rearrange("a (h p) c -> (a p) h c", p=P)
                               ).then_inc(s_w[par], 16)

            def split_expert(e, par):
                pool.wait_ge(s_whi, 2 * (e + 1))
                hi = gu_w[:, bass.ds(e * 4 * HID, 2 * HID)].bitcast(F32)
                lo = gu_w[:, bass.ds(e * 4 * HID + 2 * HID, 2 * HID)]
                nc.gpsimd.tensor_tensor(out=lo, in0=stage[:, par, 0:2 * HID], in1=hi,
                                        op=ALU.subtract).then_inc(s_wlo, 1)
                nc.gpsimd.tensor_tensor(out=down_part(e, 1),
                                        in0=stage[:, par, 2 * HID:3 * HID]
                                        .rearrange("p (h c) -> p h c", c=D),
                                        in1=down_part(e, 0).bitcast(F32),
                                        op=ALU.subtract).then_inc(s_wlo, 1)

            load_expert(0, 0)
            load_expert(1, 1)
            with pool.Fori(0, E // 2 - 1) as it:
                for par in range(2):
                    split_expert(2 * it + par, par)
                    pool.wait_ge(s_wlo, 2 * (2 * it + par + 1))
                    load_expert(2 * it + par + 2, par)

            def scatter(b):
                for t in range(b * S, (b + 1) * S):
                    for k in range(TOPK):
                        pool.indirect_dma_start(
                            sorted_x[b // BG],
                            bass.IndirectOffsetOnAxis(ap=rows[:, k, t:t + 1], axis=0),
                            xn[:, t * D:(t + 1) * D], None).then_inc(s_sc[b % 2], 16)
                if b % BG > 0:
                    confirm(s_sc, s_scb, b - 1)
                if b % BG == BG - 1:
                    confirm(s_sc, s_scb, b)

            def confirm(landed, batches, b):
                pool.wait_ge(landed[b % 2], 16 * TOPK * S * (b // 2 + 1))
                pool.sem_inc(batches, 1)

            for par in range(2):
                split_expert(E - 2 + par, par)
            def group_placed(g):
                pool.wait_ge(s_place, g + 1)
                pool.wait_ge(s_xnc, (g + 1) * NORM_STEPS // GROUPS)
                pool.wait_ge(s_zeroed[g], 16)

            def low_part(b, c, src, ready, done):
                pool.wait_ge(ready, 2 * b + c + 1)
                nc.gpsimd.tensor_tensor(out=chl[:, 1, c, :], in0=src,
                                        in1=chl[:, 0, c, :].bitcast(F32), op=ALU.subtract
                                        ).then_inc(done, 1)

            def gather(b):
                if b % BG == 0:
                    for slot in range(2):
                        pool.wait_ge(s_yst[slot], 16 * (b // BG + 1) * NQ // 2)
                if b >= RING:
                    pool.wait_ge(s_fin, b - RING + 1)
                for j in range(S):
                    for k in range(TOPK):
                        t, slot = b * S + j, ((b % RING) * S + j) * TOPK + k
                        pool.indirect_dma_start(
                            ga[:, slot * D:(slot + 1) * D], None, sorted_y[b // BG],
                            bass.IndirectOffsetOnAxis(ap=rows[:, k, t:t + 1], axis=0)
                        ).then_inc(s_gt[b % 2], 16)
                if b >= 1:
                    confirm(s_gt, s_gtb, b - 1)
                if b == B - 1:
                    confirm(s_gt, s_gtb, b)

            group_placed(0)
            for b in range(BG):
                scatter(b)
            group_placed(1)
            gathered = 0
            for b in range(HEAD, B):
                for c in range(CB):
                    low_part(b, c, vpad[:, c, PAD:PAD + T], s_yh, s_yl)
                if BG <= b - HEAD + BG < B:
                    scatter(b - HEAD + BG)
                if b - HEAD + 1 >= FIN_FIRST - 1:
                    gather(gathered)
                    gathered += 1
                for c in range(CB):
                    low_part(b, c, acc[:, c * T:(c + 1) * T], s_gvh, s_gvl)
            for b in range(gathered, B):
                gather(b)

        @block.scalar
        def _(act):
            def norm_step(s, par, first, with_experts=False):
                act.wait_ge(s_var, s + 1)
                act.activation(std, var_eps, ACT.Sqrt).then_inc(s_std, 1)
                for n in range(2 if with_experts else 0):
                    act.wait_ge(s_w[n], 48 * (s + 1))
                    act.activation(gu_w[:, bass.ds((2 * s + n) * 4 * HID, 2 * HID)],
                                   stage[:, n, 0:2 * HID], ACT.Copy).then_inc(s_whi, 1)
                    act.activation(down_part(2 * s + n, 0),
                                   stage[:, n, 2 * HID:3 * HID].rearrange("p (h c) -> p h c", c=D),
                                   ACT.Copy).then_inc(s_whi, 1)
                act.wait_ge(s_xnr, s + 1)
                act.activation(xn[:, bass.ds(s * XW * D, XW * D)], x_in[par], ACT.Copy
                               ).then_inc(s_xnc, 1)
                for h in range(2):
                    act.wait_ge(s_xt, 2 * s + h + 1)
                    if not first:
                        act.wait_ge(s_lg, 2 * s + h - 1)
                    act.activation(xn_t[h], banks[h][:, :], ACT.Copy).then_inc(s_xte, 1)
                for h in range(2):
                    act.wait_ge(s_lg, 2 * s + h + 1)
                    act.activation(logits[:, bass.ds((2 * s + h) * S * E, S * E)],
                                   banks[2 + h][:, 0:S * E], ACT.Copy).then_inc(s_lge, 1)

            def route(g):
                act.wait_ge(s_gap, g + 1)
                for k, sign in enumerate((1.0, -1.0)):
                    act.activation(rw[:, k, g * SG:(g + 1) * SG], gap, ACT.Sigmoid, scale=sign
                                   ).then_inc(s_sig, 1)
                act.wait_ge(s_nv, g + 1)
                act.activation(max1, var_n[:, g * SG:(g + 1) * SG], ACT.Sqrt).then_inc(s_nsd, 1)

            norm_step(0, 0, True, True)
            norm_step(1, 1, False, True)
            with act.Fori(1, NORM_STEPS // 4) as it:
                for par in range(2):
                    norm_step(2 * it + par, par, False, True)
            assert NORM_STEPS // GROUPS * 2 == E
            route(0)
            with act.Fori(NORM_STEPS // 4, NORM_STEPS // 2) as it:
                for par in range(2):
                    norm_step(2 * it + par, par, False)
            route(1)
            act.wait_ge(s_params, 16 * 9)
            act.activation(decay_c, ld_c, ACT.Sigmoid).then_inc(s_dec, 1)

            def make_z(b):
                if past_first(b):
                    act.wait_ge(s_zt, b)
                else:
                    act.wait_ge(s_xnc, NORM_STEPS)
                    act.wait_ge(s_xt, 2 * NORM_STEPS)
                    act.wait_ge(s_mw, 1)
                for j in range(S):
                    last = act.activation(z[:, j * D:(j + 1) * D],
                                          xn[:, bass.ds((b * S + j) * D, D)], ACT.Copy,
                                          scale=var_n[:, bass.ds(b * S + j, 1)])
                last.then_inc(s_z, 1)

            def z_hi(b):
                act.wait_ge(s_zt, b + 1)
                if past_first(b):
                    act.wait_ge(s_g, 2 * b)
                act.activation(zhl[:, 0, :], banks[MC][:, :], ACT.Copy).then_inc(s_zh, 1)

            def v_out(b, c):
                act.wait_ge(s_v, 2 * b + c + 1)
                if past_first(b):
                    act.wait_ge(s_yl, 2 * b + c - 1)
                act.activation(vpad[:, c, PAD:PAD + T], banks[MA + c][:, :], ACT.Identity,
                               bias=bias_c[:, CB + c:CB + c + 1]).then_inc(s_ve, 1)

            def first_tap(b, c):
                act.wait_ge(s_ve, 2 * b + c + 1)
                if past_first(b):
                    act.wait_ge(s_gvl, 2 * b + c - 1)
                act.activation(acc[:, c * T:(c + 1) * T], vpad[:, c, 0:T], ACT.Identity,
                               scale=dww_c[:, c * K:c * K + 1], bias=addb_c[:, c:c + 1]
                               ).then_inc(s_t0, 1)

            def make_gate(b, c):
                act.wait_ge(s_g, 2 * b + c + 1)
                if past_first(b):
                    act.wait_ge(s_gv, 2 * b + c - 1)
                act.activation(gate[:, c, :], banks[MA + c][:, :], ACT.Tanh, scale=0.5,
                               bias=bias_c[:, c:c + 1]).then_inc(s_ge, 1)

            def state_hi(b, c):
                act.wait_ge(s_y, 2 * b + c + 1)
                if past_first(b):
                    act.wait_ge(s_o, b)
                act.activation(chl[:, 0, c, :], vpad[:, c, PAD:PAD + T], ACT.Copy
                               ).then_inc(s_yh, 1)

            def gated_hi(b, c):
                act.wait_ge(s_mx, 2 * b + 2)
                act.wait_ge(s_gv, 2 * b + c + 1)
                act.activation(chl[:, 0, c, :], acc[:, c * T:(c + 1) * T], ACT.Copy
                               ).then_inc(s_gvh, 1)

            def out_copy(b):
                act.wait_ge(s_o, b + 1)
                if past_first(b):
                    act.wait_ge(s_ot, b)
                act.activation(mixed_t[:, :], banks[MC][:, :], ACT.Identity, bias=outb_c
                               ).then_inc(s_oe, 1)

            def mixer_piece(b, n):
                if n == 1:
                    make_gate(b, 0)
                elif n == 4:
                    make_gate(b, 1)
                elif n == 7:
                    state_hi(b, 0)
                elif n == 6 and past_first(b):
                    out_copy(b - 1)
                elif n == 9 and more(b):
                    make_z(b + 1)
                elif n == 15:
                    state_hi(b, 1)
                elif n == 16 and more(b):
                    z_hi(b + 1)
                elif n == 22:
                    gated_hi(b, 0)
                elif n == 25:
                    gated_hi(b, 1)
                elif n in (27, 28) and more(b):
                    v_out(b + 1, n - 27)
                elif n in (29, 30) and more(b):
                    first_tap(b + 1, n - 29)

            def batch_in(b):
                act.wait_ge(s_out, 16 * b + 16)
                act.dma_start(x_back.rearrange("p (j d) -> p j d", d=D),
                              x_v[bass.ds(b, 1)].rearrange("a p j d -> (a p) j d")
                              ).then_inc(s_xb, 16)

            def batch_out(b):
                act.wait_ge(s_fin, b + 1)
                act.dma_start(out_v[bass.ds(b, 1)].rearrange("a p j d -> (a p) j d"),
                              x_back.rearrange("p (j d) -> p j d", d=D)).then_inc(s_out, 16)

            def final_silu(b):
                act.wait_ge(s_fc, b + 1)
                v = ga[:, bass.ds((b % RING) * S * TOPK * D, S * TOPK * D)] \
                    .rearrange("p (j k d) -> p j k d", j=S, k=TOPK)[:, :, 0, :]
                act.activation(v, v, ACT.Silu).then_inc(s_fsi, 1)

            def combine_piece(b, n):
                if n == 12:
                    batch_in(b)
                elif n == 26:
                    final_silu(b)
                elif n == 31:
                    batch_out(b)

            make_z(0)
            z_hi(0)
            for c in range(CB):
                v_out(0, c)
                first_tap(0, c)
            for b in range(HEAD):
                for n in range(32):
                    mixer_piece(b, n)

            def x_hi(i, par, ends):
                act.wait_ge(s_fx, i + 1)
                if not ends or i >= 2:
                    act.wait_ge(s_fu, i - 1)
                act.activation(xhl[:, par, 0, :], banks[XT][:, 0:P], ACT.Copy).then_inc(s_fxh, 1)

            def expert_step(i, k, ends, mix, fin):
                def beside(slot):
                    if mix is not None:
                        mixer_piece(mix, 4 * k + slot)
                    if fin is not None:
                        combine_piece(fin, 4 * k + slot)

                nxt, prev, old = i + 1, i - 1, i - 2
                if not ends or nxt < TILES:
                    x_hi(nxt, (k + 1) % 2, ends)
                beside(0)
                if not ends or i < TILES:
                    act.wait_ge(s_fg, i + 1)
                    if not ends or i >= 2:
                        act.wait_ge(s_ft, i - 1)
                    act.activation(silu_h[:, k % 2, :], banks[GP][:, :], ACT.Silu
                                   ).then_inc(s_fs, 1)
                beside(1)
                if not ends or 0 <= prev < TILES:
                    act.wait_ge(s_ft, prev + 1)
                    if not ends or prev >= 2:
                        act.wait_ge(s_fy, prev - 1)
                    act.activation(hhl[:, (k - 1) % 2, 0, :], banks[HT][:, :], ACT.Copy
                                   ).then_inc(s_fhh, 1)
                beside(2)
                if not ends or 0 <= old < TILES:
                    slot, sub = ((k - 2) // QT) % 2, (k - 2) % QT
                    act.wait_ge(s_fy, old + 1)
                    if sub == 0 and (not ends or old >= 2 * QT):
                        act.wait_ge(s_yst[slot], 16 * (old // (2 * QT)) if ends
                                    else 2 * (old - 4 * slot))
                    act.activation(y_quad[:, slot, sub * D:(sub + 1) * D], banks[YP][:, 0:D],
                                   ACT.Copy).then_inc(s_fyh, 1)
                beside(3)
                if isinstance(mix, int) and k == 7:
                    out_copy(mix)

            act.sem_inc(s_out, 16)
            x_hi(0, 0, True)
            experts_schedule(act.Fori, expert_step)
            with act.Fori(FIN_IN, B) as b:
                batch_in(b)
                final_silu(b)
                batch_out(b)
            act.wait_ge(s_out, 16 * B + 16)

        @block.vector
        def _(dve):
            V = nc.vector
            link = Linked(dve, s_dconst)
            link(V.memset(ones_f, 1.0))
            link(V.memset(minus1, -1.0))
            link(V.tensor_tensor_scan(out=ramp, data0=ones_f.to_broadcast([P, E]),
                                      data1=minus1.to_broadcast([P, E]), initial=float(E + 1),
                                      op0=ALU.mult, op1=ALU.add))
            dve.wait_ge(s_tri, 2)
            V.tensor_copy(tri, tri_f[:, 0:P]).then_inc(s_tri, 1)
            V.tensor_copy(ones_r, tri_f[:, P:2 * P]).then_inc(s_tri, 1)

            norm = Linked(dve, s_n)
            NORM_LINKS = 12

            def norm_step(s, par):
                norm.base, norm.n = s * NORM_LINKS, 0
                xs = x_in[par]
                dve.wait_ge(s_x[par], 32 * ((s - par) // 2 + 1) if isinstance(s, int)
                            else 16 * (s - par) + 32)
                for j in range(XW):
                    last = V.bn_stats(stats[:, j, :], xs[:, j * D:(j + 1) * D])
                norm(last)
                mean, var = meanvar[:, 0, :], meanvar[:, 1, :]
                V.tensor_tensor(out=mean, in0=stats[:, :, 1], in1=stats[:, :, 4], op=ALU.add)
                V.tensor_tensor(out=newton, in0=stats[:, :, 1], in1=stats[:, :, 4],
                                op=ALU.subtract)
                norm(V.tensor_tensor(out=var, in0=stats[:, :, 2], in1=stats[:, :, 5], op=ALU.add))
                V.tensor_scalar(out=mean, in0=mean, scalar1=0.5, scalar2=None, op0=ALU.mult)
                norm(V.tensor_tensor(out=newton, in0=newton, in1=newton, op=ALU.mult))
                norm(V.scalar_tensor_tensor(out=var, in0=newton, scalar=D / 4, in1=var,
                                            op0=ALU.mult, op1=ALU.add))
                norm(V.tensor_scalar(out=var, in0=var, scalar1=1.0 / D, scalar2=None,
                                     op0=ALU.mult))
                V.tensor_scalar(out=var_eps, in0=var, scalar1=EPS, scalar2=None,
                                op0=ALU.add).then_inc(s_var, 1)
                dve.wait_ge(s_std, s + 1)
                norm(V.reciprocal(rstd, std))
                norm(V.tensor_tensor(out=newton, in0=rstd, in1=rstd, op=ALU.mult))
                norm(V.tensor_tensor(out=newton, in0=newton, in1=var_eps, op=ALU.mult))
                norm(V.tensor_scalar(out=newton, in0=newton, scalar1=-0.5, scalar2=1.5,
                                     op0=ALU.mult, op1=ALU.add))
                norm(V.tensor_tensor(out=rstd, in0=rstd, in1=newton, op=ALU.mult))
                for j in range(XW):
                    last = V.tensor_scalar(out=xs[:, j * D:(j + 1) * D],
                                           in0=xs[:, j * D:(j + 1) * D],
                                           scalar1=mean[:, j:j + 1], scalar2=rstd[:, j:j + 1],
                                           op0=ALU.subtract, op1=ALU.mult)
                last.then_inc(s_xnr, 1)
                norm(V.tensor_tensor(out=newton, in0=rstd, in1=rstd, op=ALU.mult))
                norm(V.tensor_tensor(out=var_n[:, bass.ds(s * XW, XW)], in0=newton,
                                     in1=var, op=ALU.mult))
                assert norm.n == NORM_LINKS

            link = Linked(dve, s_r)

            def by_tile(a, n=E):
                return a.rearrange("p (t a) -> p t a", a=1).to_broadcast([P, SG, n])

            def pick(values, largest, marks):
                link(V.tensor_reduce(out=largest, in_=values, axis=AX.X, op=ALU.max))
                link(V.tensor_tensor(out=same, in0=values, in1=by_tile(largest), op=ALU.is_equal))
                link(V.tensor_tensor(out=same, in0=same,
                                     in1=ramp.rearrange("p (a e) -> p a e", a=1)
                                     .to_broadcast([P, SG, E]), op=ALU.mult))
                link(V.tensor_reduce(out=code_max, in_=same, axis=AX.X, op=ALU.max))
                link(V.tensor_tensor(out=marks, in0=same, in1=by_tile(code_max), op=ALU.is_equal))

            def route(g):
                lg = logits[:, g * GW:(g + 1) * GW].rearrange("p (t e) -> p t e", e=E)
                dve.wait_ge(s_lge, (g + 1) * BG)
                pick(lg, max1, first_e)
                link(V.scalar_tensor_tensor(out=rest, in0=first_e, scalar=-3e38, in1=lg,
                                            op0=ALU.mult, op1=ALU.add))
                pick(rest, max2, second_e)
                V.tensor_tensor(out=picked.rearrange("p (t e) -> p t e", e=E), in0=first_e,
                                in1=second_e, op=ALU.add).then_inc(s_pick, 1)
                V.tensor_tensor(out=gap, in0=max1, in1=max2, op=ALU.subtract).then_inc(s_gap, 1)
                link(V.tensor_scalar(out=var_n[:, g * SG:(g + 1) * SG],
                                     in0=var_n[:, g * SG:(g + 1) * SG], scalar1=EPS, scalar2=None,
                                     op0=ALU.add))
                dve.sem_inc(s_nv, 1)
                dve.wait_ge(s_cnt, g + 1)
                link(V.tensor_copy(per_tile, banks[4][:, 0:GW].rearrange("p (t e) -> p e t", e=E)))
                flat = [v.rearrange("p e t -> p (e t)") for v in (per_tile, running, before)]
                link(V.tensor_tensor_scan(out=flat[1], data0=ones_f.to_broadcast([P, GW]),
                                          data1=flat[0], initial=0.0, op0=ALU.mult, op1=ALU.add))
                link(V.tensor_tensor(out=flat[2], in0=flat[1], in1=flat[0], op=ALU.subtract))
                link(V.tensor_tensor(out=n_e, in0=running[:, :, SG - 1], in1=before[:, :, 0],
                                     op=ALU.subtract))
                link(V.tensor_scalar(out=ints[:, 0:E], in0=n_e, scalar1=float(P - 1), scalar2=None,
                                     op0=ALU.add))
                link(V.tensor_scalar(out=ints[:, 0:E], in0=ints[:, 0:E], scalar1=7, scalar2=None,
                                     op0=ALU.arith_shift_right))
                link(V.tensor_copy(tiles_e, ints[:, 0:E]))
                link(V.tensor_tensor_scan(out=ends_e, data0=ones_f.to_broadcast([P, E]),
                                          data1=tiles_e, initial=0.0, op0=ALU.mult, op1=ALU.add))
                link(V.tensor_tensor(out=base_e, in0=ends_e, in1=tiles_e, op=ALU.subtract))
                link(V.scalar_tensor_tensor(out=base_e, in0=base_e, scalar=float(P),
                                            in1=before[:, :, 0], op0=ALU.mult, op1=ALU.subtract))
                link(V.tensor_tensor(out=place, in0=before,
                                     in1=base_e.rearrange("p (e a) -> p e a", a=1)
                                     .to_broadcast([P, E, SG]), op=ALU.add))
                link(V.tensor_tensor(out=place, in0=place,
                                     in1=banks[5][:, 0:GW].rearrange("p (t e) -> p e t", e=E),
                                     op=ALU.add))
                for k, marks in enumerate((first_e, second_e)):
                    link(V.tensor_tensor(out=same, in0=marks,
                                         in1=place.rearrange("p e t -> p t e"), op=ALU.mult))
                    link(V.tensor_reduce(out=code_max, in_=same, axis=AX.X, op=ALU.add))
                    i0, i1, i2 = (ints[:, n * SG:(n + 1) * SG] for n in range(3))
                    link(V.tensor_copy(i0, code_max))
                    link(V.tensor_scalar(out=i1, in0=i0, scalar1=P - 1, scalar2=2,
                                         op0=ALU.bitwise_and, op1=ALU.logical_shift_left))
                    link(V.tensor_scalar(out=i2, in0=i0, scalar1=7, scalar2=QT - 1,
                                         op0=ALU.logical_shift_right, op1=ALU.bitwise_and))
                    link(V.tensor_scalar(out=i0, in0=i0, scalar1=9, scalar2=9,
                                         op0=ALU.logical_shift_right, op1=ALU.logical_shift_left))
                    link(V.tensor_tensor(out=i0, in0=i0, in1=i1, op=ALU.bitwise_or))
                    link(V.tensor_tensor(out=rows[:, k, g * SG:(g + 1) * SG], in0=i0.bitcast(U32),
                                         in1=i2.bitcast(U32), op=ALU.bitwise_or))
                dve.sem_inc(s_place, 1)
                link(V.tensor_tensor_scan(out=tile_no, data0=ones_f.to_broadcast([P, NT]),
                                          data1=ones_f.to_broadcast([P, NT]), initial=0.0,
                                          op0=ALU.mult, op1=ALU.add))
                link(V.tensor_tensor(out=past,
                                     in0=ends_e.rearrange("p (a e) -> p a e", a=1)
                                     .to_broadcast([P, NT, E]),
                                     in1=tile_no.rearrange("p (t a) -> p t a", a=1)
                                     .to_broadcast([P, NT, E]), op=ALU.is_lt))
                link(V.tensor_reduce(out=n_past, in_=past, axis=AX.X, op=ALU.add))
                link(V.tensor_scalar(out=tile_expert[:, g * NT:(g + 1) * NT], in0=n_past,
                                     scalar1=float(E - 1), scalar2=None, op0=ALU.min))
                dve.wait_ge(s_sig, 2 * (g + 1))
                both = rw[:, :, g * SG:(g + 1) * SG]
                link(V.tensor_scalar(out=both, in0=both, scalar1=DEPTH_SCALE, scalar2=None,
                                     op0=ALU.mult))
                dve.wait_ge(s_nsd, g + 1)
                v = var_n[:, g * SG:(g + 1) * SG]
                link(V.reciprocal(max2, max1))
                link(V.tensor_tensor(out=gap, in0=max2, in1=max2, op=ALU.mult))
                link(V.tensor_tensor(out=gap, in0=gap, in1=v, op=ALU.mult))
                link(V.tensor_scalar(out=gap, in0=gap, scalar1=-0.5, scalar2=1.5, op0=ALU.mult,
                                     op1=ALU.add))
                link(V.tensor_tensor(out=v, in0=max2, in1=gap, op=ALU.mult))

            half = NORM_STEPS // 4
            for g in range(GROUPS):
                with dve.Fori(g * half, (g + 1) * half) as it:
                    for par in range(2):
                        norm_step(2 * it + par, par)
                route(g)

            link = Linked(dve, s_prep)
            dve.wait_ge(s_params, 16 * 9)
            dve.wait_ge(s_mixraw, 16 * 3)
            dve.wait_ge(s_bmm, 1)
            link(V.tensor_tensor(out=bias_c, in0=inb_c, in1=banks[6][:, 0:4], op=ALU.add))
            link(V.tensor_tensor(out=addb_c, in0=dwb_c, in1=mixb_c, op=ALU.add))
            link(V.tensor_scalar(out=inw_raw, in0=inw_raw, scalar1=gamma_c, scalar2=None,
                                 op0=ALU.mult))
            link(V.tensor_scalar(out=outw_raw, in0=outw_raw, scalar1=0.5, scalar2=None,
                                 op0=ALU.mult))
            link(V.tensor_scalar(out=bias_c[:, 0:CB], in0=bias_c[:, 0:CB], scalar1=0.5,
                                 scalar2=None, op0=ALU.mult))
            for raw, w in ((inw_raw, inw[:, :, :]),
                           (mixw_raw, mixw[:, :, :, :].rearrange("p l c n -> p l (c n)")),
                           (outw_raw, outw[:, :, :, :].rearrange("p l c n -> p l (c n)"))):
                link(V.tensor_copy(w[:, 0], raw))
                link(V.tensor_tensor(out=w[:, 1], in0=raw, in1=w[:, 0].bitcast(F32),
                                     op=ALU.subtract))
            dve.wait_ge(s_lg, 2 * NORM_STEPS)
            link(V.memset(vpad[:, :, 0:PAD], 0.0))
            dve.sem_inc(s_mw, 1)

            LINKS = CB * (K - 1) + CB

            def z_lo(b):
                dve.wait_ge(s_zh, b + 1)
                V.tensor_tensor(out=zhl[:, 1, :], in0=banks[MC][:, :],
                                in1=zhl[:, 0, :].bitcast(F32), op=ALU.subtract).then_inc(s_zl, 1)

            def tap(b, c, k):
                if k == 1:
                    dve.wait_ge(s_t0, 2 * b + c + 1)
                else:
                    dve.wait_ge(s_c, b * LINKS + c * (K - 1) + k - 1)
                a = acc[:, c * T:(c + 1) * T]
                V.scalar_tensor_tensor(out=a, in0=vpad[:, c, k:k + T],
                                       scalar=dww_c[:, c * K + k:c * K + k + 1], in1=a,
                                       op0=ALU.mult, op1=ALU.add).then_inc(s_c, 1)

            def scan(b, c):
                dve.wait_ge(s_c, b * LINKS + (c + 1) * (K - 1))
                v = vpad[:, c, PAD:PAD + T]
                V.tensor_tensor_scan(out=v, data0=decay_c[:, c:c + 1].to_broadcast([P, T]),
                                     data1=v, initial=0.0, op0=ALU.mult, op1=ALU.add
                                     ).then_inc(s_y, 1)

            def add_mix(b, c):
                a = acc[:, c * T:(c + 1) * T]
                dve.wait_ge(s_mx, 2 * b + c + 1)
                V.tensor_tensor(out=a, in0=a, in1=banks[MA + c][:, :], op=ALU.add).then_inc(s_c, 1)

            def apply_gate(b, c):
                a = acc[:, c * T:(c + 1) * T]
                dve.wait_ge(s_ge, 2 * b + c + 1)
                dve.wait_ge(s_c, b * LINKS + CB * (K - 1) + c + 1)
                V.scalar_tensor_tensor(out=a, in0=gate[:, c, :], scalar=1.0, in1=a,
                                       op0=ALU.add, op1=ALU.mult).then_inc(s_gv, 1)

            def low_part(b, c, src, ready, done):
                dve.wait_ge(ready, 2 * b + c + 1)
                V.tensor_tensor(out=chl[:, 1, c, :], in0=src, in1=chl[:, 0, c, :].bitcast(F32),
                                op=ALU.subtract).then_inc(done, 1)

            def s_out(b):
                dve.wait_ge(s_ot, b + 1)
                dve.wait_ge(s_scb, b + 1)
                v = xn[:, bass.ds(b * S * D, S * D)]
                V.tensor_tensor(out=v, in0=v, in1=banks[MC][:, :], op=ALU.add).then_inc(s_s, 1)

            def mixer_piece(b, n, alone=False):
                if n == 10 and past_first(b):
                    s_out(b - 1)
                if n < 6:
                    tap(b, 0, n + 1)
                elif n == 6:
                    scan(b, 0)
                elif n < 13:
                    tap(b, 1, n - 6)
                elif n == 13:
                    scan(b, 1)
                elif n == 16 and alone:
                    for c in range(CB):
                        low_part(b, c, vpad[:, c, PAD:PAD + T], s_yh, s_yl)
                elif n == 17 and more(b):
                    z_lo(b + 1)
                elif n == 20:
                    add_mix(b, 0)
                elif n == 21:
                    apply_gate(b, 0)
                elif n == 23:
                    add_mix(b, 1)
                elif n == 24:
                    apply_gate(b, 1)
                elif n == 26 and alone:
                    for c in range(CB):
                        low_part(b, c, acc[:, c * T:(c + 1) * T], s_gvh, s_gvl)

            combine_steps = Linked(dve, s_f)

            def combine(b):
                combine_steps.base, combine_steps.n = b * 2, 0
                dve.wait_ge(s_gtb, b + 1)
                v = ga[:, bass.ds((b % RING) * S * TOPK * D, S * TOPK * D)] \
                    .rearrange("p (j k d) -> p j k d", j=S, k=TOPK)
                for j in range(S):
                    last = V.tensor_scalar(out=v[:, j, 0, :], in0=v[:, j, 0, :],
                                           scalar1=rw[:, 0, bass.ds(b * S + j, 1)], scalar2=None,
                                           op0=ALU.mult)
                combine_steps(last)
                for j in range(S):
                    last = V.scalar_tensor_tensor(out=v[:, j, 0, :], in0=v[:, j, 1, :],
                                                  scalar=rw[:, 1, bass.ds(b * S + j, 1)],
                                                  in1=v[:, j, 0, :], op0=ALU.mult, op1=ALU.add)
                last.then_inc(s_fc, 1)

            def finish(b):
                combine_steps.base, combine_steps.n = b * 2 + 1, 0
                dve.wait_ge(s_fsi, b + 1)
                dve.wait_ge(s_s, b + 1)
                v = ga[:, bass.ds((b % RING) * S * TOPK * D, S * TOPK * D)] \
                    .rearrange("p (j k d) -> p j k d", j=S, k=TOPK)[:, :, 0, :]
                s_b = xn[:, bass.ds(b * S * D, S * D)].rearrange("p (j d) -> p j d", d=D)
                combine_steps(V.tensor_tensor(out=v, in0=v, in1=s_b, op=ALU.mult))
                dve.wait_ge(s_xb, 16 * (b + 1))
                xb = x_back.rearrange("p (j d) -> p j d", d=D)
                V.tensor_tensor(out=xb, in0=xb, in1=v, op=ALU.add).then_inc(s_fin, 1)

            def combine_piece(b, n):
                if n == 22:
                    combine(b)
                elif n == 29:
                    finish(b)

            dve.wait_ge(s_dec, 1)
            z_lo(0)
            for b in range(HEAD):
                for n in range(32):
                    mixer_piece(b, n, True)

            def x_lo(i, par):
                dve.wait_ge(s_fxh, i + 1)
                V.tensor_tensor(out=xhl[:, par, 1, :], in0=banks[XT][:, 0:P],
                                in1=xhl[:, par, 0, :].bitcast(F32), op=ALU.subtract
                                ).then_inc(s_fxl, 1)

            def expert_step(i, k, ends, mix, fin):
                def beside(slot):
                    if mix is not None:
                        mixer_piece(mix, 4 * k + slot)
                    if fin is not None:
                        combine_piece(fin, 4 * k + slot)

                if not ends or i + 1 < TILES:
                    x_lo(i + 1, (k + 1) % 2)
                beside(0)
                if not ends or i < TILES:
                    h = silu_h[:, k % 2, :]
                    dve.wait_ge(s_fs, i + 1)
                    dve.wait_ge(s_fu, i + 1)
                    V.tensor_tensor(out=h, in0=h, in1=banks[UP][:, :], op=ALU.mult
                                    ).then_inc(s_fh, 1)
                beside(1)
                if not ends or 0 <= i - 1 < TILES:
                    par = (k - 1) % 2
                    dve.wait_ge(s_fhh, i)
                    V.tensor_tensor(out=hhl[:, par, 1, :], in0=banks[HT][:, :],
                                    in1=hhl[:, par, 0, :].bitcast(F32), op=ALU.subtract
                                    ).then_inc(s_fhl, 1)
                beside(2)
                if not ends or 0 <= i - 2 < TILES:
                    slot, sub = ((k - 2) // QT) % 2, (k - 2) % QT
                    y = y_quad[:, slot, sub * D:(sub + 1) * D]
                    dve.wait_ge(s_fyh, i - 1)
                    V.tensor_tensor(out=y, in0=y, in1=banks[YP][:, D:2 * D], op=ALU.add
                                    ).then_inc(s_fye, 1)
                beside(3)
                if isinstance(mix, int) and k == 7:
                    s_out(mix)

            x_lo(0, 0)
            experts_schedule(dve.Fori, expert_step)
            with dve.Fori(FIN_IN, B) as b:
                combine(b)
                finish(b)

        @block.tensor
        def _(pe):
            mm = nc.tensor.matmul

            def three(out_ps, stat, mov, start, stop):
                mm(out_ps, stat[0], mov[0], start=start, stop=False)
                mm(out_ps, stat[0], mov[1], start=False, stop=False)
                return mm(out_ps, stat[1], mov[0], start=False, stop=stop)

            def norm_step(s, par, first):
                pe.wait_ge(s_xnr, s + 1)
                for h in range(2):
                    if not first:
                        pe.wait_ge(s_xte, 2 * s + h - 1)
                    for j in range(S):
                        t = h * S + j
                        last = nc.tensor.transpose(banks[h][:, j * P:(j + 1) * P],
                                                   x_in[par][:, t * D:(t + 1) * D], ident[:, :])
                    last.then_inc(s_xt, 1)
                for h in range(2):
                    pe.wait_ge(s_xte, 2 * s + h + 1)
                    if not first:
                        pe.wait_ge(s_lge, 2 * s + h - 1)
                    for j in range(S):
                        last = mm(banks[2 + h][:, j * E:(j + 1) * E], xn_t[h][:, j * P:(j + 1) * P],
                                  route_w[:, :], start=True, stop=True)
                    last.then_inc(s_lg, 1)

            def count(g):
                pe.wait_ge(s_pick, g + 1)
                if g:
                    pe.wait_ge(s_place, g)
                mm(banks[4][:, 0:GW], ones_r, picked, start=True, stop=True)
                mm(banks[5][:, 0:GW], tri, picked, start=True, stop=True).then_inc(s_cnt, 1)

            pe.wait_ge(s_const, 2)
            pe.wait_ge(s_params, 16 * 9)
            pe.wait_ge(s_tri, 4)
            norm_step(0, 0, True)
            norm_step(1, 1, False)
            with pe.Fori(1, NORM_STEPS // 4) as it:
                for par in range(2):
                    norm_step(2 * it + par, par, False)
            count(0)
            with pe.Fori(NORM_STEPS // 4, NORM_STEPS // 2) as it:
                for par in range(2):
                    norm_step(2 * it + par, par, False)
            count(1)
            pe.wait_ge(s_mixraw, 48)
            for n in range(2 * CB):
                last = mm(banks[6][:, n:n + 1], inw_raw[:, n * P:(n + 1) * P], beta_c,
                          start=True, stop=True)
            last.then_inc(s_bmm, 1)

            def z_turn(b):
                pe.wait_ge(s_z, b + 1)
                if not past_first(b):
                    pe.wait_ge(s_mw, 1)
                elif not isinstance(b, int) or b > 1:
                    pe.wait_ge(s_s, b - 1)
                else:
                    pe.wait_ge(s_zl, 1)
                for j in range(S):
                    last = nc.tensor.transpose(banks[MC][:, j * P:(j + 1) * P],
                                               z[:, j * D:(j + 1) * D], ident[:, :])
                last.then_inc(s_zt, 1)

            def project(b, c, kind, done):
                n = (kind * CB + c) * P
                three(banks[MA + c][:, :], [inw[:, l, n:n + P] for l in range(2)],
                      [zhl[:, l, :] for l in range(2)], True, True).then_inc(done, 1)

            def project_v(b, c):
                pe.wait_ge(s_zl, b + 1)
                if past_first(b):
                    pe.wait_ge(s_gv, 2 * b + c - 1)
                project(b, c, 1, s_v)

            def project_g(b, c):
                pe.wait_ge(s_ve, 2 * b + c + 1)
                project(b, c, 0, s_g)

            def mix(b, m):
                pe.wait_ge(s_yl, 2 * b + 2)
                pe.wait_ge(s_ge, 2 * b + m + 1)
                for c in range(CB):
                    last = three(banks[MA + m][:, :],
                                 [mixw[:, l, c, m * P:(m + 1) * P] for l in range(2)],
                                 [chl[:, l, c, :] for l in range(2)], c == 0, c == CB - 1)
                last.then_inc(s_mx, 1)

            def out_product(b):
                pe.wait_ge(s_gvl, 2 * b + 2)
                if more(b):
                    pe.wait_ge(s_zl, b + 2)
                else:
                    pe.wait_ge(s_s, b)
                for c in range(CB):
                    last = three(banks[MC][:, :], [outw[:, l, c, :] for l in range(2)],
                                 [chl[:, l, c, :] for l in range(2)], c == 0, c == CB - 1)
                last.then_inc(s_o, 1)

            def out_turn(b):
                pe.wait_ge(s_oe, b + 1)
                for j in range(S):
                    last = nc.tensor.transpose(banks[MC][:, j * D:(j + 1) * D],
                                               mixed_t[:, j * P:(j + 1) * P], ident[:, :])
                last.then_inc(s_ot, 1)

            def mixer_piece(b, n):
                if n == 0:
                    project_g(b, 1)
                elif n == 2 and past_first(b):
                    out_product(b - 1)
                elif n == 4 and past_first(b):
                    out_turn(b - 1)
                elif n == 6 and more(b):
                    z_turn(b + 1)
                elif n in (9, 10):
                    mix(b, n - 9)
                elif n in (12, 13) and more(b):
                    project_v(b + 1, n - 12)
                elif n == 15 and more(b):
                    project_g(b + 1, 0)

            z_turn(0)
            for c in range(CB):
                project_v(0, c)
            project_g(0, 0)
            for b in range(HEAD):
                for n in range(16):
                    mixer_piece(b, n)

            def x_turn(i, k, ends):
                slot, sub = (k // QT) % 2, k % QT
                if sub == 0:
                    pe.wait_ge(s_q[slot], 16 * (i // (2 * QT) + 1) if ends
                               else 2 * (i - 4 * slot) + 16)
                if not ends or i >= 1:
                    pe.wait_ge(s_fxl, i)
                nc.tensor.transpose(banks[XT][:, 0:P], x_quad[:, slot, sub * P:(sub + 1) * P],
                                    ident[:, :]).then_inc(s_fx, 1)

            def expert_step(i, k, ends, mix, fin):
                if not ends or i + 1 < TILES:
                    x_turn(i + 1, (k + 1) % 8, ends)
                if not ends or i < TILES:
                    w = pe.snap(expert_of[k % 8], min_val=0, max_val=E - 1) * (4 * HID)
                    pe.wait_ge(s_fxl, i + 1)
                    for half, bank, done, emptied in ((0, GP, s_fg, s_fs), (1, UP, s_fu, s_fh)):
                        if not ends or i >= 1:
                            pe.wait_ge(emptied, i)
                        three(banks[bank][:, :],
                              [xhl[:, k % 2, l, :] for l in range(2)],
                              [gu_w[:, bass.ds(w + l * 2 * HID + half * HID, HID)]
                               for l in range(2)], True, True).then_inc(done, 1)
                if not ends or i + 1 < TILES:
                    pe.reg_load(expert_of[(k + 1) % 8], tile_expert[0:1, bass.ds(i + 1, 1)])
                if mix is not None:
                    mixer_piece(mix, 2 * k)
                if not ends or 0 <= i - 1 < TILES:
                    par = (k - 1) % 2
                    pe.wait_ge(s_fh, i)
                    if not ends or i - 1 >= 1:
                        pe.wait_ge(s_fhl, i - 1)
                    for n in range(HB):
                        last = nc.tensor.transpose(banks[HT][:, n * P:(n + 1) * P],
                                                   silu_h[:, par, n * P:(n + 1) * P], ident[:, :])
                    last.then_inc(s_ft, 1)
                if not ends or 0 <= i - 2 < TILES:
                    par = k % 2
                    w = pe.snap(expert_of[(k - 2) % 8], min_val=0, max_val=E - 1) * (2 * HID)
                    pe.wait_ge(s_fhl, i - 1)
                    if not ends or i - 2 >= 1:
                        pe.wait_ge(s_fye, i - 2)
                    for n in range(HB):
                        wn = w + n * 2 * D
                        mm(banks[YP][:, 0:2 * D], hhl[:, par, 0, n * P:(n + 1) * P],
                           dn_w[:, bass.ds(wn, 2 * D)], start=(n == 0), stop=False)
                        last = mm(banks[YP][:, 0:D], hhl[:, par, 1, n * P:(n + 1) * P],
                                  dn_w[:, bass.ds(wn, D)], start=False, stop=(n == HB - 1))
                    last.then_inc(s_fy, 1)
                if mix is not None:
                    mixer_piece(mix, 2 * k + 1)
                if isinstance(mix, int) and k == 7:
                    out_product(mix)
                    out_turn(mix)

            expert_of = [pe.alloc_register(f"expert_of_{k}") for k in range(8)]
            pe.wait_ge(s_wlo, 2 * E)
            pe.wait_ge(s_s, 1)
            pe.reg_load(expert_of[0], tile_expert[0:1, 0:1])
            x_turn(0, 0, True)
            experts_schedule(pe.Fori, expert_step)


_INS = ['L0_attn_x', 'L0_attn_norm_gamma', 'L0_attn_norm_beta', 'L0_attn_in_w', 'L0_attn_in_b',
        'L0_attn_dw_w', 'L0_attn_dw_b', 'L0_attn_log_decay', 'L0_attn_mix_w', 'L0_attn_mix_b',
        'L0_attn_out_w', 'L0_attn_out_b', 'L0_ffn_Wr', 'L0_ffn_Wg', 'L0_ffn_Wu', 'L0_ffn_Wd']


def kernel(**inputs):
    import numpy as _np
    import concourse.bacc as _bacc
    from concourse import mybir as _mybir
    from concourse.bass_utils import run_bass_kernel_spmd as _run

    nc = _bacc.Bacc("TRN2", target_bir_lowering=False, num_devices=1)
    arrays, args = {}, []
    for name in _INS:
        a = _np.ascontiguousarray(inputs[name])
        arrays[f"in_{name}_dram"] = a
        args.append(nc.dram_tensor(f"in_{name}_dram", a.shape, _mybir.dt.from_np(a.dtype),
                                   kind="ExternalInput").ap())
    shape = arrays["in_L0_attn_x_dram"].shape
    args.append(nc.dram_tensor("out_dram", shape, _mybir.dt.float32, kind="ExternalOutput").ap())
    recurrent_moe_block(nc, *args)
    r = _run(nc, [arrays], core_ids=[0])
    return r.results[0]["out_dram"]
```

```python
import concourse.bass as bass
from concourse import mybir
from contextlib import ExitStack


def recurrent_moe_block(nc, x, gamma, beta, in_w, in_b, dw_w, dw_b, log_decay, mix_w, mix_b,
                        out_w, out_b, w_route, w_gate, w_up, w_down, out):
    F32, F32R, I32, U32 = mybir.dt.float32, mybir.dt.float32r, mybir.dt.int32, mybir.dt.uint32
    ALU, ACT, AX = mybir.AluOpType, mybir.ActivationFunctionType, mybir.AxisListType

    P = 128
    B, T, D = x.shape
    H = in_w.shape[1] // 2
    K = dw_w.shape[1]
    E, _, HID = w_gate.shape
    TOPK = 2
    PAD = K - 1
    CB = H // P
    HB = HID // P
    S = T // P
    NS = B * S
    GROUP_B = (12, B - 12)
    GROUPS = len(GROUP_B)
    G0 = [sum(GROUP_B[:g]) for g in range(GROUPS + 1)]
    SG = [S * n for n in GROUP_B]
    SG_MAX = max(SG)
    QT = 4
    NT = [-(-(n * TOPK + E - 1) // 8) * 8 for n in SG]
    T0 = [sum(NT[:g]) for g in range(GROUPS + 1)]
    NQ = [n // QT for n in NT]
    TILES = sum(NT)
    EPS = 1e-5
    DEPTH_SCALE = 1.0 / (12 ** 0.5)
    ITERS = TILES // 8
    HEAD = 3
    EARLY = 16
    MIX_LAST = B - 1 - HEAD
    FIN_FIRST = T0[1] // 8 + 1
    FIN_IN = 2 * (ITERS - FIN_FIRST)
    assert GROUPS == 2 and MIX_LAST + 1 < FIN_FIRST
    RING = 5
    RING_OWN = 3
    BATCH_ROWS = S * TOPK * D
    assert RING * BATCH_ROWS <= RING_OWN * BATCH_ROWS + 4 * T

    x_v = x.rearrange("b (j p) d -> b p j d", p=P)
    out_v = out.rearrange("b (j p) d -> b p j d", p=P)
    sorted_x = [nc.dram_tensor(f"sorted_x{g}", [NT[g] * P, D], F32, kind="Internal").ap()
                for g in range(GROUPS)]
    sorted_y = [nc.dram_tensor(f"sorted_y{g}", [NT[g] * P, D], F32, kind="Internal").ap()
                for g in range(GROUPS)]
    sx_v = [v.rearrange("(q p s) d -> q p (s d)", p=P, s=QT) for v in sorted_x]
    sy_v = [v.rearrange("(q p s) d -> q p (s d)", p=P, s=QT) for v in sorted_y]

    ctx = ExitStack()
    with ctx:
        def sb(name, shape, dt=F32):
            return ctx.enter_context(nc.sbuf_tensor(name, shape, dt))

        def sem(name):
            return ctx.enter_context(nc.semaphore(name))

        xn = sb("xn", [P, NS * D])
        gu_w = sb("gu_w", [P, E * 2 * 2 * HID], F32R)
        dn_w = sb("dn_w", [P, E * 2 * HB * D], F32R)
        inw = sb("inw", [P, 2, 2 * H], F32R)
        mixw = sb("mixw", [P, 2, CB, H], F32R)
        outw = sb("outw", [P, 2, CB, D], F32R)
        ident = sb("ident", [P, P])
        route_w = sb("route_w", [P, E])
        rows = sb("rows", [P, TOPK, NS], U32)
        rw = sb("rw", [P, TOPK, NS])
        tile_expert = sb("tile_expert", [P, TILES], I32)
        var_n = sb("var_n", [P, NS])
        params = sb("params", [P, 64])
        gamma_c, beta_c = params[:, 0:1], params[:, 1:2]
        inb_c, bias_c = params[:, 2:6], params[:, 6:10]
        dww_c = params[:, 10:10 + CB * K]
        dwb_c, mixb_c, addb_c = params[:, 24:26], params[:, 26:28], params[:, 28:30]
        ld_c, decay_c = params[:, 30:32], params[:, 32:34]
        ramp = params[:, 34:42]
        outb_c = params[:, 44:45]
        ones_f = params[:, 42:43]
        minus1 = params[:, 43:44]
        work = sb("work", [P, 6 * HID])
        stage = work[:, :].rearrange("p (r n) -> p r n", r=2)
        silu_h = work[:, 0:2 * HID].rearrange("p (r n) -> p r n", r=2)
        x_quad = work[:, 2 * HID:4 * HID].rearrange("p (r n) -> p r n", r=2)
        y_quad = work[:, 4 * HID:6 * HID].rearrange("p (r n) -> p r n", r=2)
        xhl = sb("xhl", [P, 2, 2, P], F32R)
        hhl = sb("hhl", [P, 2, 2, HID], F32R)
        zhl = sb("zhl", [P, 2, T], F32R)
        vpad = sb("vpad", [P, CB, PAD + T])
        shared = sb("shared", [P, RING_OWN * BATCH_ROWS + 3 * T + CB * T])
        ga = shared[:, 0:RING * BATCH_ROWS]
        acc = shared[:, RING_OWN * BATCH_ROWS:RING_OWN * BATCH_ROWS + 3 * T]
        chl = sb("chl", [P, 2, CB, T], F32R)
        gates = shared[:, RING_OWN * BATCH_ROWS + 3 * T:]
        gate = gates[:, :].rearrange("p (c t) -> p c t", c=CB)
        logits, inw_raw = gates[:, 0:NS * E], gates[:, NS * E:NS * E + 2 * H]
        mixed_t = sb("mixed_t", [P, T])
        xr = sb("xr", [P, 2 * T])
        ffn = [mixed_t[:, :], gates[:, T:2 * T]]
        x_back = [xr[:, 0:T], xr[:, T:2 * T]]
        z = xr[:, T:2 * T]
        x_norm = [xr[:, :], acc[:, 0:2 * T]]
        xn_t = [vpad[:, 0, 0:T], vpad[:, 1, 0:T]]
        tri = zhl[:, 0, 0:P]
        ones_r = zhl[:, 0, P:2 * P]
        picked = chl[:, 0, 0, 0:SG_MAX * E]
        at = [0]

        def scratch(*shape):
            n = 1
            for s in shape:
                n *= s
            v = ga[:, at[0]:at[0] + n]
            at[0] += n
            assert at[0] <= RING_OWN * BATCH_ROWS
            return v if len(shape) == 1 else v.rearrange("p (a b) -> p a b", a=shape[0])

        mixw_raw, outw_raw = mixed_t[:, :], acc[:, 2 * T:2 * T + CB * D]
        tri_f = scratch(2 * P)
        same_m = scratch(SG_MAX * E)
        marks_at = at[0]
        first_m, second_m, rest_m = (scratch(SG_MAX * E) for _ in range(3))
        max1_m, max2_m, code_max_m, gap_m = (scratch(SG_MAX) for _ in range(4))
        codes = scratch(TOPK * SG_MAX)
        running_m, before_m = (scratch(SG_MAX * E) for _ in range(2))
        n_e, tiles_e, ends_e, base_e = (scratch(E) for _ in range(4))
        tile_no_m = scratch(max(NT))
        ints, ints_e = before_m.bitcast(I32), tile_no_m[:, 0:E].bitcast(I32)
        assert max(NT) <= 3 * SG_MAX and 3 * TOPK <= E
        small = sb("small", [P, 136])
        stats = small[:, 0:48].rearrange("p (j k) -> p j k", k=6)
        meanvar = [small[:, n:n + 16].rearrange("p (k j) -> p k j", k=2) for n in (48, 64)]
        var_eps = [small[:, 80:88], small[:, 88:96]]
        std = [small[:, 96:104], small[:, 104:112]]
        rstd, newton, apart = small[:, 112:120], small[:, 120:128], small[:, 128:136]

        XT, GP, UP, HT, YP, MA, MB, MC = range(8)
        banks = [ctx.enter_context(nc.psum_tensor(f"bank{k}", [P, 512], F32)) for k in range(8)]

        s_params = sem("params_loaded")
        s_mixraw = sem("mixer_weights_loaded")
        s_x = [sem("x_loaded_0"), sem("x_loaded_1")]
        s_const = sem("constants_built")
        s_tri = sem("triangle_built")
        s_dconst = sem("vector_constants")
        s_zero = sem("zeros_built")
        s_zeroed = [sem(f"sorted_x{g}_zeroed") for g in range(GROUPS)]
        s_w = [sem("expert_loaded_0"), sem("expert_loaded_1")]
        s_whi = sem("expert_hi")
        s_wlo = sem("expert_lo")
        s_n = sem("statistics_steps")
        s_nf = sem("norm_steps")
        s_var = sem("variance_ready")
        s_std = sem("std_ready")
        s_xnr = sem("xn_ready")
        s_xnc = sem("xn_kept")
        s_xt = sem("xn_transposed")
        s_xte = sem("xn_t_ready")
        s_lg = sem("logits_summed")
        s_lge = sem("logits_ready")
        s_r = sem("route_steps")
        s_pick = sem("experts_picked")
        s_cnt = sem("pairs_counted")
        s_gap = sem("logit_gap")
        s_sig = sem("expert_weights")
        s_nv = sem("xn_variance_eps")
        s_nsd = sem("xn_std")
        s_place = sem("places_ready")
        s_sc = [sem("scatter_even"), sem("scatter_odd")]
        s_scb = sem("batches_scattered")
        s_prep = sem("bias_steps")
        s_mws = sem("mixer_weight_steps")
        s_bmm = sem("bias_product")
        s_dec = sem("decay_ready")
        s_mw = sem("mixer_weights_ready")
        s_q = [sem("x_quad_loaded_0"), sem("x_quad_loaded_1")]
        s_fx = sem("tile_transposed")
        s_fxh = sem("tile_hi")
        s_fxl = sem("tile_lo")
        s_fg = sem("gate_product")
        s_fu = sem("up_product")
        s_fs = sem("silu_ready")
        s_fh = sem("hidden_ready")
        s_ft = sem("hidden_transposed")
        s_fhh = sem("hidden_hi")
        s_fhl = sem("hidden_lo")
        s_fy = sem("down_product")
        s_fyh = sem("y_half")
        s_fye = sem("y_ready")
        s_yst = [sem("y_quad_stored_0"), sem("y_quad_stored_1")]
        s_z = sem("z_ready")
        s_zt = sem("z_transposed")
        s_zh = sem("z_hi")
        s_zl = sem("z_lo")
        s_v = sem("v_product")
        s_g = sem("g_product")
        s_ve = sem("v_ready")
        s_ge = sem("gate_ready")
        s_t0 = sem("first_tap")
        s_c = sem("taps_added")
        s_am = sem("mix_added")
        s_y = sem("state_ready")
        s_yh = sem("state_hi")
        s_yl = sem("state_lo")
        s_mx = sem("mix_product")
        s_gv = sem("gated_sum")
        s_gvh = sem("gated_hi")
        s_gvl = sem("gated_lo")
        s_o = sem("out_product")
        s_oe = sem("out_copied")
        s_ot = sem("out_transposed")
        s_s = sem("s_ready")
        s_gt = [sem("gather_even"), sem("gather_odd")]
        s_gtb = sem("batches_gathered")
        s_xb = [sem("x_back_loaded_0"), sem("x_back_loaded_1")]
        s_f = sem("ffn_times_s")
        s_y0 = sem("first_rows_weighted")
        s_fc = sem("ffn_combined")
        s_fsi = sem("ffn_silu")
        s_fin = sem("result_ready")
        s_out = [sem("result_stored_0"), sem("result_stored_1")]

        def counts(g):
            gw = SG[g] * E
            assert g == 0 or 2 * gw <= 512
            return banks[4][:, 0:gw], banks[5][:, 0:gw] if g == 0 else banks[4][:, gw:2 * gw]

        block = ctx.enter_context(nc.Block())

        class Linked:

            def __init__(self, engine, counter):
                self.engine, self.counter, self.base, self.n = engine, counter, 0, 0

            def __call__(self, instruction, wait=True):
                self.n += 1
                instruction.then_inc(self.counter, 1)
                if wait:
                    self.wait()

            def wait(self):
                self.engine.wait_ge(self.counter, self.base + self.n)

        def down_part(e, half):
            return dn_w[:, bass.ds(e * 2 * HID, 2 * HID)] \
                .rearrange("p (h l c) -> p h l c", h=HB, l=2)[:, :, half, :]

        XW = 2 * S
        NORM_STEPS = B // 2
        GROUP_STEPS = [n // 2 for n in GROUP_B]
        WEIGHT_STEPS = 8

        def experts_schedule(fori, step):
            def iteration(it, ends, mix, fin):
                for k in range(8):
                    step(it * 8 + k, k, ends, mix, fin)

            iteration(0, True, HEAD, None)
            with fori(1, MIX_LAST - 1) as it:
                iteration(it, False, it + HEAD, None)
            for it in range(MIX_LAST - 1, FIN_FIRST):
                iteration(it, True, it + HEAD, None)
            with fori(FIN_FIRST, ITERS - 1) as it:
                iteration(it, False, None, it - FIN_FIRST)
            iteration(ITERS - 1, True, None, ITERS - 1 - FIN_FIRST)
            for k in range(2):
                step(TILES + k, k, True, None, None)

        def is_batch(b):
            return not isinstance(b, int) or 0 <= b < B

        def beside_slot(mix, slot):
            return mix is not None and not (isinstance(mix, int) and mix == HEAD
                                            and slot < EARLY)

        def past(b, n=1):
            return not isinstance(b, int) or b >= n

        def acc_of(b, c):
            return acc[:, bass.ds((b % 2) * T, T)] if c == 0 else acc[:, 2 * T:3 * T]

        @block.sync
        def _(sp):
            def load_x(step_, par):
                sp.dma_start(xn[:, bass.ds(step_ * XW * D, XW * D)]
                             .rearrange("p (b j d) -> p b j d", b=2, d=D),
                             x_v[bass.ds(2 * step_, 2)].rearrange("b p j d -> p b j d")
                             ).then_inc(s_x[par], 16)

            def load_expert(e, par):
                sp.dma_start(stage[:, par, 0:HID],
                             w_gate[bass.ds(e, 1)].rearrange("a p n -> (a p) n")
                             ).then_inc(s_w[par], 16)
                sp.dma_start(stage[:, par, HID:2 * HID],
                             w_up[bass.ds(e, 1)].rearrange("a p n -> (a p) n")
                             ).then_inc(s_w[par], 16)
                sp.dma_start(stage[:, par, 2 * HID:3 * HID].rearrange("p (h c) -> p h c", c=D),
                             w_down[bass.ds(e, 1)].rearrange("a (h p) c -> (a p) h c", p=P)
                             ).then_inc(s_w[par], 16)

            def zero_list(g, first, quads):
                zeros = hhl[:, 0, 0, :].bitcast(F32).rearrange("p (a n) -> p a n", a=1)
                sp.dma_start(sx_v[g][bass.ds(first, quads)].rearrange("q p n -> p q n"),
                             zeros.to_broadcast([P, quads, HID])).then_inc(s_zeroed[g], 16)

            ZERO_STEP = 6
            zero_first = NQ[0] - ZERO_STEP * (NORM_STEPS // 2 - 1)
            load_x(0, 0)
            load_x(1, 1)
            for dst, src in ((route_w[:, :], w_route),
                             (gamma_c, gamma.rearrange("(p a) -> p a", a=1)),
                             (beta_c, beta.rearrange("(p a) -> p a", a=1)),
                             (inb_c, in_b.rearrange("(c p) -> p c", p=P)),
                             (dww_c.rearrange("p (c k) -> p c k", c=CB),
                              dw_w.rearrange("(c p) k -> p c k", p=P)),
                             (dwb_c, dw_b.rearrange("(c p) -> p c", p=P)),
                             (mixb_c, mix_b.rearrange("(c p) -> p c", p=P)),
                             (ld_c, log_decay.rearrange("(c p) -> p c", p=P)),
                             (outb_c, out_b.rearrange("(p a) -> p a", a=1))):
                with nc.allow_non_contiguous_dma(reason="a few small parameters"):
                    sp.dma_start(dst, src).then_inc(s_params, 16)
            sp.dma_start(inw_raw, in_w).then_inc(s_mixraw, 16)
            sp.dma_start(mixw_raw.rearrange("p (c n) -> p c n", c=CB),
                         mix_w.rearrange("(c p) n -> p c n", p=P)).then_inc(s_mixraw, 16)
            sp.dma_start(outw_raw.rearrange("p (c n) -> p c n", c=CB),
                         out_w.rearrange("(c p) n -> p c n", p=P)).then_inc(s_mixraw, 16)
            load_expert(0, 0)
            sp.wait_ge(s_x[0], 16)
            load_x(2, 0)
            load_expert(1, 1)
            sp.wait_ge(s_x[1], 16)
            load_x(3, 1)
            for s in range(4, NORM_STEPS):
                if s == NORM_STEPS - 2:
                    sp.wait_ge(s_zero, 1)
                    zero_list(0, 0, zero_first)
                sp.wait_ge(s_x[s % 2], 16 * (s // 2))
                load_x(s, s % 2)
            for s in range(2, NORM_STEPS):
                sp.wait_ge(s_wlo, 2 * (s - 1))
                load_expert(s, s % 2)
                if s % 2 == 1:
                    zero_list(0, zero_first + ZERO_STEP * (s // 2 - 1), ZERO_STEP)
            zero_list(1, 0, NQ[1])

            def quad_in(g, q, slot, reuse):
                if reuse:
                    sp.wait_ge(s_fx, (q + (T0[g] // QT - 1)) * QT)
                sp.dma_start(x_quad[:, slot, :],
                             sx_v[g][bass.ds(q, 1)].rearrange("a p n -> (a p) n")
                             ).then_inc(s_q[slot], 16)

            def quad_out(g, q, slot):
                sp.wait_ge(s_fye, (q + (T0[g] // QT + 1)) * QT)
                sp.dma_start(sy_v[g][bass.ds(q, 1)].rearrange("a p n -> (a p) n"),
                             y_quad[:, slot, :]).then_inc(s_yst[slot], 16)

            sp.wait_ge(s_wlo, 2 * E)
            for g in range(GROUPS):
                sp.wait_ge(s_scb, G0[g + 1])
                for slot in range(2):
                    quad_in(g, slot, slot, g > 0)
                    if g:
                        quad_out(g - 1, NQ[g - 1] - 2 + slot, slot)
                with sp.Fori(1, NQ[g] // 2) as it:
                    for slot in range(2):
                        quad_in(g, 2 * it + slot, slot, True)
                        quad_out(g, 2 * it + slot - 2, slot)
            for slot in range(2):
                quad_out(GROUPS - 1, NQ[-1] - 2 + slot, slot)
            for slot in range(2):
                sp.wait_ge(s_yst[slot], 16 * sum(NQ) // 2)

        @block.gpsimd
        def _(pool):
            nc.gpsimd.memset(hhl[:, 0, 0, :].bitcast(F32), 0.0
                             ).then_inc(s_zero, 1)
            nc.gpsimd.memset(ident[:, :], 0.0).then_inc(s_const, 1)
            nc.gpsimd.memset(tri_f, 1.0).then_inc(s_tri, 1)
            pool.wait_ge(s_const, 1)
            nc.gpsimd.affine_select(out=ident[:, :], in_=ident[:, :], compare_op=ALU.not_equal,
                                    fill=1.0, base=0, pattern=[[-1, P]], channel_multiplier=1
                                    ).then_inc(s_const, 1)
            pool.wait_ge(s_tri, 1)
            nc.gpsimd.affine_select(out=tri_f[:, 0:P], in_=tri_f[:, 0:P], compare_op=ALU.is_ge,
                                    fill=0.0, base=-1, pattern=[[1, P]], channel_multiplier=-1
                                    ).then_inc(s_tri, 1)

            def split_expert(e, par):
                pool.wait_ge(s_whi, 2 * (e + 1))
                hi = gu_w[:, bass.ds(e * 4 * HID, 2 * HID)].bitcast(F32)
                lo = gu_w[:, bass.ds(e * 4 * HID + 2 * HID, 2 * HID)]
                nc.gpsimd.tensor_tensor(out=lo, in0=stage[:, par, 0:2 * HID], in1=hi,
                                        op=ALU.subtract).then_inc(s_wlo, 1)
                nc.gpsimd.tensor_tensor(out=down_part(e, 1),
                                        in0=stage[:, par, 2 * HID:3 * HID]
                                        .rearrange("p (h c) -> p h c", c=D),
                                        in1=down_part(e, 0).bitcast(F32),
                                        op=ALU.subtract).then_inc(s_wlo, 1)

            step = Linked(pool, s_mws)
            pool.wait_ge(s_mixraw, 16 * 3)
            pool.wait_ge(s_bmm, 1)
            step(nc.gpsimd.tensor_scalar(out=inw_raw, in0=inw_raw, scalar1=gamma_c, scalar2=None,
                                         op0=ALU.mult))
            step(nc.gpsimd.tensor_scalar(out=outw_raw, in0=outw_raw, scalar1=0.5, scalar2=None,
                                         op0=ALU.mult))
            for raw, w in ((inw_raw, inw[:, :, :]),
                           (mixw_raw, mixw[:, :, :, :].rearrange("p l c n -> p l (c n)")),
                           (outw_raw, outw[:, :, :, :].rearrange("p l c n -> p l (c n)"))):
                step(nc.gpsimd.tensor_copy(w[:, 0], raw))
                step(nc.gpsimd.tensor_tensor(out=w[:, 1], in0=raw, in1=w[:, 0].bitcast(F32),
                                             op=ALU.subtract))
            assert step.n == WEIGHT_STEPS
            with pool.Fori(0, E // 2 - 1) as it:
                for par in range(2):
                    split_expert(2 * it + par, par)

            def group_of(b):
                return 0 if b < G0[1] else 1

            def scatter(b, tiles=range(S)):
                for j in tiles:
                    for k in range(TOPK):
                        t = b * S + j
                        pool.indirect_dma_start(
                            sorted_x[group_of(b)],
                            bass.IndirectOffsetOnAxis(ap=rows[:, k, t:t + 1], axis=0),
                            xn[:, t * D:(t + 1) * D], None).then_inc(s_sc[b % 2], 16)
                if tiles[-1] == S - 1:
                    if b not in G0:
                        confirm(s_sc, s_scb, b - 1)
                    if b + 1 in G0:
                        confirm(s_sc, s_scb, b)

            def confirm(landed, batches, b):
                pool.wait_ge(landed[b % 2], 16 * TOPK * S * (b // 2 + 1))
                pool.sem_inc(batches, 1)

            def group_placed(g):
                pool.wait_ge(s_place, g + 1)
                pool.wait_ge(s_xnc, sum(GROUP_STEPS[:g + 1]))
                zero_parts = NORM_STEPS // 2 if g == 0 else 1
                pool.wait_ge(s_zeroed[g], 16 * zero_parts)

            def low_part(b, c, src, ready, done):
                pool.wait_ge(ready, 2 * b + c + 1)
                nc.gpsimd.tensor_tensor(out=chl[:, 1, c, :], in0=src,
                                        in1=chl[:, 0, c, :].bitcast(F32), op=ALU.subtract
                                        ).then_inc(done, 1)

            def gather(b):
                if b in G0:
                    for slot in range(2):
                        pool.wait_ge(s_yst[slot], 16 * T0[group_of(b) + 1] // QT // 2)
                if b == RING_OWN:
                    pool.wait_ge(s_s, B)
                if b >= RING:
                    pool.wait_ge(s_fc, b - RING + 1)
                for j in range(S):
                    for k in range(TOPK):
                        t, slot = b * S + j, ((b % RING) * S + j) * TOPK + k
                        pool.indirect_dma_start(
                            ga[:, slot * D:(slot + 1) * D], None, sorted_y[group_of(b)],
                            bass.IndirectOffsetOnAxis(ap=rows[:, k, t:t + 1], axis=0)
                        ).then_inc(s_gt[b % 2], 16)
                if b >= 1:
                    confirm(s_gt, s_gtb, b - 1)
                if b == B - 1:
                    confirm(s_gt, s_gtb, b)

            group_placed(0)
            for b in range(G0[1]):
                scatter(b)
            group_placed(1)
            for b in range(HEAD, B):
                to_scatter = b - HEAD + G0[1]
                for c in range(CB):
                    low_part(b, c, vpad[:, c, PAD:PAD + T], s_yh, s_yl)
                if to_scatter < B:
                    scatter(to_scatter, range(S // 2))
                for c in range(CB):
                    low_part(b, c, acc_of(b, c), s_gvh, s_gvl)
                if to_scatter < B:
                    scatter(to_scatter, range(S // 2, S))
            for b in range(B):
                gather(b)

        @block.scalar
        def _(act):
            def deviation(s, par):
                act.wait_ge(s_var, s + 1)
                act.activation(std[par], var_eps[par], ACT.Sqrt).then_inc(s_std, 1)

            def norm_step(s, par, before_logits, first=False, last=False):
                if not last:
                    deviation(s + 1, 1 - par)
                for h in range(2):
                    act.wait_ge(s_xt, 2 * s + h + 1)
                    if not first:
                        act.wait_ge(s_lg, 2 * s + h - 1)
                    act.activation(xn_t[h], banks[h][:, :], ACT.Copy).then_inc(s_xte, 1)
                act.wait_ge(s_xnr, s + 1)
                act.activation(xn[:, bass.ds(s * XW * D, XW * D)], x_norm[par], ACT.Copy
                               ).then_inc(s_xnc, 1)
                if before_logits is not None:
                    expert_hi(before_logits, 1 - par)
                for h in range(2):
                    act.wait_ge(s_lg, 2 * s + h + 1)
                    act.activation(logits[:, bass.ds((2 * s + h) * S * E, S * E)],
                                   banks[2 + h][:, 0:S * E], ACT.Copy).then_inc(s_lge, 1)

            def expert_hi(e, par):
                act.wait_ge(s_w[par], 48 * ((e - par) // 2 + 1) if isinstance(e, int)
                            else 24 * (e - par) + 48)
                act.activation(gu_w[:, bass.ds(e * 4 * HID, 2 * HID)], stage[:, par, 0:2 * HID],
                               ACT.Copy).then_inc(s_whi, 1)
                act.activation(down_part(e, 0),
                               stage[:, par, 2 * HID:3 * HID].rearrange("p (h c) -> p h c", c=D),
                               ACT.Copy).then_inc(s_whi, 1)

            def route(g):
                tiles = slice(G0[g] * S, G0[g + 1] * S)
                act.wait_ge(s_gap, g + 1)
                for k, sign in enumerate((1.0, -1.0)):
                    act.activation(rw[:, k, tiles], gap_m[:, 0:SG[g]], ACT.Sigmoid, scale=sign
                                   ).then_inc(s_sig, 1)
                act.wait_ge(s_nv, g + 1)
                act.activation(max1_m[:, 0:SG[g]], var_n[:, tiles], ACT.Sqrt).then_inc(s_nsd, 1)

            assert NORM_STEPS == E
            deviation(0, 0)
            norm_step(0, 0, None, first=True)
            norm_step(1, 1, 0)
            with act.Fori(1, GROUP_STEPS[0] // 2) as it:
                for par in range(2):
                    norm_step(2 * it + par, par, 2 * it + (par - 1))
            expert_hi(E - 3, 1)
            act.wait_ge(s_params, 16 * 9)
            act.activation(decay_c, ld_c, ACT.Sigmoid).then_inc(s_dec, 1)
            route(0)
            for par in range(2):
                expert_hi(E - 2 + par, par)
            norm_step(NORM_STEPS - 2, 0, None)
            norm_step(NORM_STEPS - 1, 1, None, last=True)

            def make_z(b, j):
                if j == 0 and past(b):
                    act.wait_ge(s_zt, b)
                elif j == 0:
                    act.wait_ge(s_xnc, NORM_STEPS)
                    act.wait_ge(s_mw, 1)
                act.activation(z[:, j * D:(j + 1) * D], xn[:, bass.ds((b * S + j) * D, D)],
                               ACT.Copy, scale=var_n[:, bass.ds(b * S + j, 1)]
                               ).then_inc(s_z, 1)

            def z_hi(b):
                act.wait_ge(s_zt, b + 1)
                if past(b):
                    act.wait_ge(s_g, 2 * b)
                else:
                    act.wait_ge(s_cnt, GROUPS)
                act.activation(zhl[:, 0, :], banks[MC][:, :], ACT.Copy).then_inc(s_zh, 1)

            def v_out(b, c):
                act.wait_ge(s_v, 2 * b + c + 1)
                if past(b):
                    act.wait_ge(s_yl, 2 * b + c - 1)
                act.activation(vpad[:, c, PAD:PAD + T], banks[MA + c][:, :], ACT.Identity,
                               bias=bias_c[:, CB + c:CB + c + 1]).then_inc(s_ve, 1)

            def first_tap(b, c):
                act.wait_ge(s_ve, 2 * b + c + 1)
                if past(b, 2 - c):
                    act.wait_ge(s_gvl, 2 * b - 3 if c == 0 else 2 * b)
                act.activation(acc_of(b, c), vpad[:, c, 0:T], ACT.Identity,
                               scale=dww_c[:, c * K:c * K + 1], bias=addb_c[:, c:c + 1]
                               ).then_inc(s_t0, 1)

            def make_gate(b, c):
                act.wait_ge(s_g, 2 * b + c + 1)
                if past(b):
                    act.wait_ge(s_gv, 2 * b + c - 1)
                act.activation(gate[:, c, :], banks[MA + c][:, :], ACT.Tanh, scale=0.5,
                               bias=bias_c[:, c:c + 1]).then_inc(s_ge, 1)

            def state_hi(b, c):
                act.wait_ge(s_y, 2 * b + c + 1)
                if past(b):
                    act.wait_ge(s_o, b)
                act.activation(chl[:, 0, c, :], vpad[:, c, PAD:PAD + T], ACT.Copy
                               ).then_inc(s_yh, 1)

            def gated_hi(b, c):
                act.wait_ge(s_mx, 2 * b + 2)
                act.wait_ge(s_gv, 2 * b + c + 1)
                act.activation(chl[:, 0, c, :], acc_of(b, c), ACT.Copy
                               ).then_inc(s_gvh, 1)

            def out_copy(b):
                act.wait_ge(s_o, b + 1)
                if past(b):
                    act.wait_ge(s_ot, b)
                act.activation(mixed_t[:, :], banks[MC][:, :], ACT.Identity, bias=outb_c
                               ).then_inc(s_oe, 1)

            def mixer_piece(b, n):
                if n == 1 and is_batch(b + 1):
                    z_hi(b + 1)
                elif n == 2 and is_batch(b):
                    make_gate(b, 1)
                elif n == 8 and is_batch(b - 1):
                    out_copy(b - 1)
                elif n == 9 and is_batch(b):
                    state_hi(b, 0)
                elif n == 14 and is_batch(b + 1):
                    v_out(b + 1, 0)
                elif n == 12 and is_batch(b):
                    state_hi(b, 1)
                elif n == 15 and is_batch(b + 1):
                    first_tap(b + 1, 0)
                elif n in (16, 17, 18, 19) and is_batch(b + 2):
                    make_z(b + 2, n - 16)
                elif n == 22 and is_batch(b):
                    gated_hi(b, 0)
                elif n == 24 and is_batch(b):
                    gated_hi(b, 1)
                elif n == 25 and is_batch(b + 1):
                    make_gate(b + 1, 0)
                elif n == 27 and is_batch(b + 1):
                    v_out(b + 1, 1)
                elif n == 30 and is_batch(b + 1):
                    first_tap(b + 1, 1)

            def gathered(b):
                return ga[:, bass.ds((b % RING) * BATCH_ROWS, BATCH_ROWS)] \
                    .rearrange("p (j k d) -> p j k d", j=S, k=TOPK)

            def batch_in(q, par):
                act.wait_ge(s_out[par], 16 * q + 16)
                act.dma_start(x_back[par].rearrange("p (j d) -> p j d", d=D),
                              x_v[bass.ds(2 * q + par, 1)].rearrange("a p j d -> (a p) j d")
                              ).then_inc(s_xb[par], 16)

            def weigh_first(q, par, tiles=range(S)):
                b = 2 * q + par
                if tiles[0] == 0:
                    act.wait_ge(s_gtb, b + 1)
                v = gathered(b)
                for j in tiles:
                    act.activation(v[:, j, 0, :], v[:, j, 0, :], ACT.Copy,
                                   scale=rw[:, 0, bass.ds(b * S + j, 1)]).then_inc(s_y0, 1)

            def final_silu(q, par):
                act.wait_ge(s_fc, 2 * q + par + 1)
                act.activation(ffn[par], ffn[par], ACT.Silu).then_inc(s_fsi, 1)

            def batch_out(q, par):
                b = 2 * q + par
                act.wait_ge(s_fin, b + 1)
                act.dma_start(out_v[bass.ds(b, 1)].rearrange("a p j d -> (a p) j d"),
                              x_back[par].rearrange("p (j d) -> p j d", d=D)
                              ).then_inc(s_out[par], 16)

            def combine_piece(q, n):
                par, m = n // 16, n % 16
                if m == 0:
                    batch_in(q, par)
                elif m in (2, 3):
                    weigh_first(q, par, range(S // 2 * (m - 2), S // 2 * (m - 1)))
                elif m == 7:
                    final_silu(q, par)
                elif m == 14:
                    batch_out(q, par)

            for j in range(S):
                make_z(0, j)
            for n in range(16):
                mixer_piece(-1, n)
            route(1)
            for n in range(16, 32):
                mixer_piece(-1, n)
            for b in range(HEAD):
                for n in range(32):
                    mixer_piece(b, n)
            for n in range(EARLY):
                mixer_piece(HEAD, n)

            def x_hi(i, par, ends):
                act.wait_ge(s_fx, i + 1)
                if not ends or i >= 2:
                    act.wait_ge(s_fu, i - 1)
                act.activation(xhl[:, par, 0, :], banks[XT][:, 0:P], ACT.Copy).then_inc(s_fxh, 1)

            def expert_step(i, k, ends, mix, fin):
                def beside(slot):
                    if beside_slot(mix, 4 * k + slot):
                        mixer_piece(mix, 4 * k + slot)
                    if fin is not None:
                        combine_piece(fin, 4 * k + slot)

                nxt, prev, old = i + 1, i - 1, i - 2
                if not ends or nxt < TILES:
                    x_hi(nxt, (k + 1) % 2, ends)
                beside(0)
                if not ends or i < TILES:
                    act.wait_ge(s_fg, i + 1)
                    if not ends or i >= 2:
                        act.wait_ge(s_ft, i - 1)
                    act.activation(silu_h[:, k % 2, :], banks[GP][:, :], ACT.Silu
                                   ).then_inc(s_fs, 1)
                beside(1)
                if not ends or 0 <= prev < TILES:
                    act.wait_ge(s_ft, prev + 1)
                    if not ends or prev >= 2:
                        act.wait_ge(s_fy, prev - 1)
                    act.activation(hhl[:, (k - 1) % 2, 0, :], banks[HT][:, :], ACT.Copy
                                   ).then_inc(s_fhh, 1)
                beside(2)
                if not ends or 0 <= old < TILES:
                    slot, sub = ((k - 2) // QT) % 2, (k - 2) % QT
                    act.wait_ge(s_fy, old + 1)
                    if sub == 0 and (not ends or old >= 2 * QT):
                        act.wait_ge(s_yst[slot], 16 * (old // (2 * QT)) if ends
                                    else 2 * (old - 4 * slot))
                    act.activation(y_quad[:, slot, sub * D:(sub + 1) * D], banks[YP][:, 0:D],
                                   ACT.Copy).then_inc(s_fyh, 1)
                beside(3)

            for par in range(2):
                act.sem_inc(s_out[par], 16)
            x_hi(0, 0, True)
            experts_schedule(act.Fori, expert_step)
            with act.Fori(FIN_IN // 2, B // 2 - 1) as q:
                for par in range(2):
                    batch_in(q, par)
                for piece in (weigh_first, final_silu, batch_out):
                    for par in range(2):
                        piece(q, par)
            q = B // 2 - 1
            for par in range(2):
                batch_in(q, par)
            for par in range(2):
                weigh_first(q, par)
                if par == 0:
                    final_silu(q, par)
            for half in range(2):
                act.wait_ge(s_fc, B + half)
                v = ffn[1][:, half * (T // 2):(half + 1) * (T // 2)]
                act.activation(v, v, ACT.Silu).then_inc(s_fsi, 1)
            batch_out(q, 0)
            act.wait_ge(s_fin, B + 1)
            batch_out(q, 1)
            for par in range(2):
                act.wait_ge(s_out[par], 16 * (B // 2) + 16)

        @block.vector
        def _(dve):
            V = nc.vector
            link = Linked(dve, s_dconst)
            link(V.memset(ones_f, 1.0))
            link(V.memset(minus1, -1.0))
            link(V.tensor_tensor_scan(out=ramp, data0=ones_f.to_broadcast([P, E]),
                                      data1=minus1.to_broadcast([P, E]), initial=float(E + 1),
                                      op0=ALU.mult, op1=ALU.add))
            dve.wait_ge(s_tri, 2)
            V.tensor_copy(tri, tri_f[:, 0:P]).then_inc(s_tri, 1)
            V.tensor_copy(ones_r, tri_f[:, P:2 * P]).then_inc(s_tri, 1)

            norm = Linked(dve, s_n)
            STAT_LINKS, NORM_LINKS = 4, 5
            scaled = Linked(dve, s_nf)

            def stage_1(s, par, prev=True, stat=True):
                if stat:
                    norm.base, norm.n = s * STAT_LINKS, 0
                    dve.wait_ge(s_x[par], 16 * ((s - par) // 2 + 1) if isinstance(s, int)
                                else 8 * (s - par) + 16)
                    for j in range(XW):
                        last = V.bn_stats(stats[:, j, :], xn[:, bass.ds((s * XW + j) * D, D)])
                    norm(last, wait=False)
                if prev:
                    scaled.base, scaled.n = s * NORM_LINKS - NORM_LINKS, 0
                    old = 1 - par
                    old_mean, old_var = meanvar[old][:, 0, :], meanvar[old][:, 1, :]
                    dve.wait_ge(s_std, s)
                    scaled(V.reciprocal(rstd, std[old]), wait=False)
                if stat:
                    mean, var = meanvar[par][:, 0, :], meanvar[par][:, 1, :]
                    norm.wait()
                    V.tensor_tensor(out=mean, in0=stats[:, :, 1], in1=stats[:, :, 4], op=ALU.add)
                    V.tensor_tensor(out=apart, in0=stats[:, :, 1], in1=stats[:, :, 4],
                                    op=ALU.subtract)
                    norm(V.tensor_tensor(out=var, in0=stats[:, :, 2], in1=stats[:, :, 5],
                                         op=ALU.add), wait=False)
                if prev:
                    scaled.wait()
                    scaled(V.tensor_tensor(out=newton, in0=rstd, in1=rstd, op=ALU.mult),
                           wait=False)
                if stat:
                    norm.wait()
                    V.tensor_scalar(out=mean, in0=mean, scalar1=0.5, scalar2=None, op0=ALU.mult)
                    norm(V.tensor_tensor(out=apart, in0=apart, in1=apart, op=ALU.mult),
                         wait=False)
                if prev:
                    scaled.wait()
                    scaled(V.scalar_tensor_tensor(out=newton, in0=newton, scalar=-0.5,
                                                  in1=var_eps[old], op0=ALU.mult,
                                                  op1=ALU.mult), wait=False)
                if stat:
                    norm.wait()
                    norm(V.scalar_tensor_tensor(out=var, in0=apart, scalar=D / 4, in1=var,
                                                op0=ALU.mult, op1=ALU.add), wait=False)
                if prev:
                    scaled.wait()
                    scaled(V.scalar_tensor_tensor(out=rstd, in0=newton, scalar=1.5, in1=rstd,
                                                  op0=ALU.add, op1=ALU.mult), wait=False)
                if stat:
                    norm.wait()
                    V.tensor_scalar(out=var_eps[par], in0=var, scalar1=1.0 / D, scalar2=EPS,
                                    op0=ALU.mult, op1=ALU.add).then_inc(s_var, 1)
                    assert norm.n == STAT_LINKS
                if prev:
                    scaled.wait()
                    if past(s, 3):
                        dve.wait_ge(s_xnc, s - 2)
                        dve.wait_ge(s_xt, 2 * s - 4)
                    for j in range(XW):
                        last = V.tensor_scalar(out=x_norm[old][:, j * D:(j + 1) * D],
                                               in0=xn[:, bass.ds((s * XW + (j - XW)) * D, D)],
                                               scalar1=old_mean[:, j:j + 1],
                                               scalar2=rstd[:, j:j + 1],
                                               op0=ALU.subtract, op1=ALU.mult)
                    last.then_inc(s_xnr, 1)
                    scaled(V.tensor_tensor(out=newton, in0=rstd, in1=rstd, op=ALU.mult))
                    V.tensor_tensor(out=var_n[:, bass.ds(s * XW - XW, XW)], in0=newton,
                                    in1=old_var, op=ALU.mult)
                    assert scaled.n == NORM_LINKS

            link = Linked(dve, s_r)

            def by_tile(a):
                return a.rearrange("p (t a) -> p t a", a=1).to_broadcast([P, a.shape[1], E])

            def pick(values, largest, code_max, same, marks):
                link(V.tensor_reduce(out=largest, in_=values, axis=AX.X, op=ALU.max))
                link(V.tensor_tensor(out=same, in0=values, in1=by_tile(largest), op=ALU.is_equal))
                link(V.tensor_tensor(out=same, in0=same,
                                     in1=ramp.rearrange("p (a e) -> p a e", a=1)
                                     .to_broadcast(list(same.shape)), op=ALU.mult))
                link(V.tensor_reduce(out=code_max, in_=same, axis=AX.X, op=ALU.max))
                link(V.tensor_tensor(out=marks, in0=same, in1=by_tile(code_max), op=ALU.is_equal))

            def choose(first_tile, n, at):
                same, first_e, second_e, rest = (
                    v[:, at * E:(at + n) * E].rearrange("p (t e) -> p t e", e=E)
                    for v in (same_m, first_m, second_m, rest_m))
                max1, max2, code_max = (v[:, at:at + n] for v in (max1_m, max2_m, code_max_m))
                lg = logits[:, first_tile * E:(first_tile + n) * E] \
                    .rearrange("p (t e) -> p t e", e=E)
                dve.wait_ge(s_lge, (first_tile + n) // S)
                pick(lg, max1, code_max, same, first_e)
                link(V.scalar_tensor_tensor(out=rest, in0=first_e, scalar=-3e38, in1=lg,
                                            op0=ALU.mult, op1=ALU.add))
                pick(rest, max2, code_max, same, second_e)
                link(V.tensor_tensor(out=picked[:, at * E:(at + n) * E]
                                     .rearrange("p (t e) -> p t e", e=E), in0=first_e,
                                     in1=second_e, op=ALU.add))

            def route(g, beside=None):
                n, nt = SG[g], NT[g]
                gw = n * E
                tiles = slice(G0[g] * S, G0[g + 1] * S)
                same, first_e, second_e, rest = (
                    v[:, 0:gw].rearrange("p (t e) -> p t e", e=E)
                    for v in (same_m, first_m, second_m, rest_m))
                max1, max2, gap = (v[:, 0:n] for v in (max1_m, max2_m, gap_m))
                per_tile, running, before = (v[:, 0:gw].rearrange("p (e t) -> p e t", e=E)
                                             for v in (rest_m, running_m, before_m))
                place = running
                ended = ga[:, marks_at:marks_at + nt * E].rearrange("p (a b) -> p a b", a=nt)
                tile_no = tile_no_m[:, 0:nt]
                dve.sem_inc(s_pick, 1)
                V.tensor_tensor(out=gap, in0=max1, in1=max2, op=ALU.subtract).then_inc(s_gap, 1)
                link(V.tensor_scalar(out=var_n[:, tiles], in0=var_n[:, tiles], scalar1=1.0 / D,
                                     scalar2=EPS, op0=ALU.mult, op1=ALU.add))
                dve.sem_inc(s_nv, 1)
                dve.wait_ge(s_cnt, g + 1)
                link(V.tensor_copy(per_tile, counts(g)[0].rearrange("p (t e) -> p e t", e=E)))
                flat = [v.rearrange("p e t -> p (e t)") for v in (per_tile, running, before)]
                link(V.tensor_tensor_scan(out=flat[1], data0=ones_f.to_broadcast([P, gw]),
                                          data1=flat[0], initial=0.0, op0=ALU.mult, op1=ALU.add))
                link(V.tensor_tensor(out=flat[2], in0=flat[1], in1=flat[0], op=ALU.subtract))
                if beside is not None:
                    beside()
                link(V.tensor_tensor(out=n_e, in0=running[:, :, n - 1], in1=before[:, :, 0],
                                     op=ALU.subtract))
                link(V.tensor_tensor(out=place, in0=before,
                                     in1=counts(g)[1].rearrange("p (t e) -> p e t", e=E),
                                     op=ALU.add), wait=False)
                link(V.tensor_scalar(out=ints_e, in0=n_e, scalar1=float(P - 1), scalar2=None,
                                     op0=ALU.add))
                link(V.tensor_scalar(out=ints_e, in0=ints_e, scalar1=7, scalar2=None,
                                     op0=ALU.arith_shift_right))
                link(V.tensor_copy(tiles_e, ints_e))
                link(V.tensor_tensor_scan(out=ends_e, data0=ones_f.to_broadcast([P, E]),
                                          data1=tiles_e, initial=0.0, op0=ALU.mult, op1=ALU.add))
                link(V.tensor_tensor(out=base_e, in0=ends_e, in1=tiles_e, op=ALU.subtract))
                link(V.scalar_tensor_tensor(out=base_e, in0=base_e, scalar=float(P),
                                            in1=before[:, :, 0], op0=ALU.mult, op1=ALU.subtract))
                link(V.tensor_tensor(out=place, in0=place,
                                     in1=base_e.rearrange("p (e a) -> p e a", a=1)
                                     .to_broadcast([P, E, n]), op=ALU.add))
                places = codes[:, 0:TOPK * n]
                products = (same, rest)
                for k, marks in enumerate((first_e, second_e)):
                    link(V.tensor_tensor(out=products[k], in0=marks,
                                         in1=place.rearrange("p e t -> p t e"), op=ALU.mult),
                         wait=(k == 1))
                for k in range(TOPK):
                    link(V.tensor_reduce(out=places[:, k * n:(k + 1) * n], in_=products[k],
                                         axis=AX.X, op=ALU.add), wait=(k == 1))
                i0, i1, i2 = (ints[:, m * TOPK * SG_MAX:m * TOPK * SG_MAX + TOPK * n]
                              for m in range(3))
                link(V.tensor_copy(i0, places))
                V.tensor_scalar(out=i1, in0=i0, scalar1=P - 1, scalar2=2,
                                op0=ALU.bitwise_and, op1=ALU.logical_shift_left)
                link(V.tensor_scalar(out=i2, in0=i0, scalar1=7, scalar2=QT - 1,
                                     op0=ALU.logical_shift_right, op1=ALU.bitwise_and),
                     wait=False)
                link(V.tensor_scalar(out=i0, in0=i0, scalar1=9, scalar2=9,
                                     op0=ALU.logical_shift_right, op1=ALU.logical_shift_left))
                link(V.tensor_tensor(out=i0, in0=i0, in1=i1, op=ALU.bitwise_or))
                link(V.tensor_tensor(out=rows[:, :, tiles],
                                     in0=i0.bitcast(U32).rearrange("p (k t) -> p k t", k=TOPK),
                                     in1=i2.bitcast(U32).rearrange("p (k t) -> p k t", k=TOPK),
                                     op=ALU.bitwise_or))
                dve.sem_inc(s_place, 1)
                link(V.tensor_tensor_scan(out=tile_no, data0=ones_f.to_broadcast([P, nt]),
                                          data1=ones_f.to_broadcast([P, nt]), initial=0.0,
                                          op0=ALU.mult, op1=ALU.add))
                link(V.tensor_tensor(out=ended,
                                     in0=ends_e.rearrange("p (a e) -> p a e", a=1)
                                     .to_broadcast([P, nt, E]),
                                     in1=tile_no.rearrange("p (t a) -> p t a", a=1)
                                     .to_broadcast([P, nt, E]), op=ALU.is_lt))
                link(V.tensor_reduce(out=tile_no, in_=ended, axis=AX.X, op=ALU.add))
                link(V.tensor_scalar(out=tile_expert[:, T0[g]:T0[g + 1]], in0=tile_no,
                                     scalar1=float(E - 1), scalar2=None, op0=ALU.min))
                dve.wait_ge(s_sig, 2 * (g + 1))
                both = rw[:, :, tiles]
                link(V.tensor_scalar(out=both, in0=both, scalar1=DEPTH_SCALE, scalar2=None,
                                     op0=ALU.mult))
                dve.wait_ge(s_nsd, g + 1)
                v = var_n[:, tiles]
                link(V.reciprocal(max2, max1))
                link(V.tensor_tensor(out=gap, in0=max2, in1=max2, op=ALU.mult))
                link(V.tensor_tensor(out=gap, in0=gap, in1=v, op=ALU.mult))
                link(V.tensor_scalar(out=gap, in0=gap, scalar1=-0.5, scalar2=1.5, op0=ALU.mult,
                                     op1=ALU.add))
                link(V.tensor_tensor(out=v, in0=max2, in1=gap, op=ALU.mult))

            stage_1(0, 0, prev=False)
            stage_1(1, 1)
            stage_1(2, 0)
            for s in range(3, GROUP_STEPS[0]):
                stage_1(s, s % 2)
            s = GROUP_STEPS[0]
            stage_1(s, 0, stat=False)
            stage_1(s, 0, prev=False)
            choose(0, SG[0] - XW, 0)
            choose(SG[0] - XW, XW, SG[0] - XW)
            route(0)
            stage_1(NORM_STEPS - 1, 1)
            stage_1(NORM_STEPS, 0, stat=False)

            dve.wait_ge(s_whi, 2 * E)
            for par in range(2):
                e = E - 2 + par
                hi = gu_w[:, e * 4 * HID:e * 4 * HID + 2 * HID].bitcast(F32)
                lo = gu_w[:, e * 4 * HID + 2 * HID:(e + 1) * 4 * HID]
                V.tensor_tensor(out=lo, in0=stage[:, par, 0:2 * HID], in1=hi, op=ALU.subtract
                                ).then_inc(s_wlo, 1)
                V.tensor_tensor(out=down_part(e, 1),
                                in0=stage[:, par, 2 * HID:3 * HID]
                                .rearrange("p (h c) -> p h c", c=D),
                                in1=down_part(e, 0).bitcast(F32), op=ALU.subtract
                                ).then_inc(s_wlo, 1)

            step = Linked(dve, s_prep)
            dve.wait_ge(s_params, 16 * 9)
            dve.wait_ge(s_bmm, 1)
            step(V.tensor_tensor(out=bias_c, in0=inb_c, in1=banks[6][:, 0:4], op=ALU.add))
            step(V.tensor_tensor(out=addb_c, in0=dwb_c, in1=mixb_c, op=ALU.add))
            step(V.tensor_scalar(out=bias_c[:, 0:CB], in0=bias_c[:, 0:CB], scalar1=0.5,
                                 scalar2=None, op0=ALU.mult))
            dve.wait_ge(s_lg, 2 * NORM_STEPS)
            step(V.memset(vpad[:, :, 0:PAD], 0.0))
            dve.sem_inc(s_mw, 1)

            def z_lo(b):
                dve.wait_ge(s_zh, b + 1)
                V.tensor_tensor(out=zhl[:, 1, :], in0=banks[MC][:, :],
                                in1=zhl[:, 0, :].bitcast(F32), op=ALU.subtract).then_inc(s_zl, 1)

            choose(G0[1] * S, SG[1], 0)
            route(1, lambda: z_lo(0))

            def tap(b, c, k):
                if k == 1:
                    dve.wait_ge(s_t0, 2 * b + c + 1)
                else:
                    dve.wait_ge(s_c, (2 * b + c) * (K - 1) + k - 1)
                a = acc_of(b, c)
                V.scalar_tensor_tensor(out=a, in0=vpad[:, c, k:k + T],
                                       scalar=dww_c[:, c * K + k:c * K + k + 1], in1=a,
                                       op0=ALU.mult, op1=ALU.add).then_inc(s_c, 1)

            def scan(b, c):
                dve.wait_ge(s_c, (2 * b + c + 1) * (K - 1))
                v = vpad[:, c, PAD:PAD + T]
                V.tensor_tensor_scan(out=v, data0=decay_c[:, c:c + 1].to_broadcast([P, T]),
                                     data1=v, initial=0.0, op0=ALU.mult, op1=ALU.add
                                     ).then_inc(s_y, 1)

            def add_mix(b, c):
                a = acc_of(b, c)
                dve.wait_ge(s_mx, 2 * b + c + 1)
                V.tensor_tensor(out=a, in0=a, in1=banks[MA + c][:, :], op=ALU.add
                                ).then_inc(s_am, 1)

            def apply_gate(b, c):
                a = acc_of(b, c)
                dve.wait_ge(s_ge, 2 * b + c + 1)
                dve.wait_ge(s_am, 2 * b + c + 1)
                V.scalar_tensor_tensor(out=a, in0=gate[:, c, :], scalar=1.0, in1=a,
                                       op0=ALU.add, op1=ALU.mult).then_inc(s_gv, 1)

            def low_part(b, c, src, ready, done):
                dve.wait_ge(ready, 2 * b + c + 1)
                V.tensor_tensor(out=chl[:, 1, c, :], in0=src, in1=chl[:, 0, c, :].bitcast(F32),
                                op=ALU.subtract).then_inc(done, 1)

            def s_out(b):
                dve.wait_ge(s_ot, b + 1)
                dve.wait_ge(s_scb, b + 1)
                v = xn[:, bass.ds(b * S * D, S * D)]
                V.tensor_tensor(out=v, in0=v, in1=banks[MC][:, :], op=ALU.add).then_inc(s_s, 1)

            def mixer_piece(b, n, alone=False):
                block_1 = (0, 3, 4, 6, 7, 8)
                if alone:
                    block_0, add_at, gate_at = (16, 17, 18, 21, 25, 27), (19, 22), (20, 23)
                else:
                    block_0, add_at, gate_at = (16, 20, 24, 26, 27, 28), (18, 22), (19, 23)
                if n in block_1 and is_batch(b):
                    tap(b, 1, block_1.index(n) + 1)
                elif n == 14 and is_batch(b - 1):
                    s_out(b - 1)
                elif n == 10 and is_batch(b) and alone:
                    low_part(b, 0, vpad[:, 0, PAD:PAD + T], s_yh, s_yl)
                elif n == 2 and is_batch(b) and is_batch(b + 1):
                    z_lo(b + 1)
                elif n == 11 and is_batch(b):
                    scan(b, 1)
                elif n == 15 and is_batch(b) and alone:
                    low_part(b, 1, vpad[:, 1, PAD:PAD + T], s_yh, s_yl)
                elif n in block_0 and is_batch(b + 1):
                    tap(b + 1, 0, block_0.index(n) + 1)
                elif n in add_at and is_batch(b):
                    add_mix(b, add_at.index(n))
                elif n in gate_at and is_batch(b):
                    apply_gate(b, gate_at.index(n))
                elif n in (24, 26) and is_batch(b) and alone:
                    c = (n - 24) // 2
                    low_part(b, c, acc_of(b, c), s_gvh, s_gvl)
                elif n == 30 and is_batch(b + 1):
                    scan(b + 1, 0)

            def gathered(b):
                return ga[:, bass.ds((b % RING) * BATCH_ROWS, BATCH_ROWS)] \
                    .rearrange("p (j k d) -> p j k d", j=S, k=TOPK)

            def add_second(q, par, tiles=range(S), count_half=False):
                b = 2 * q + par
                dve.wait_ge(s_y0, S * b + tiles[-1] + 1)
                v = gathered(b)
                for j in tiles:
                    last = V.scalar_tensor_tensor(out=ffn[par][:, j * D:(j + 1) * D],
                                                  in0=v[:, j, 1, :],
                                                  scalar=rw[:, 1, bass.ds(b * S + j, 1)],
                                                  in1=v[:, j, 0, :], op0=ALU.mult, op1=ALU.add)
                if tiles[-1] == S - 1 or count_half:
                    last.then_inc(s_fc, 1)

            def times_s(q, par):
                dve.wait_ge(s_fsi, 2 * q + par + 1)
                V.tensor_tensor(out=ffn[par], in0=ffn[par],
                                in1=xn[:, bass.ds((2 * q + par) * S * D, S * D)], op=ALU.mult
                                ).then_inc(s_f, 1)

            def add_x(q, par):
                dve.wait_ge(s_f, 2 * q + par + 1)
                dve.wait_ge(s_xb[par], 16 * (q + 1))
                V.tensor_tensor(out=x_back[par], in0=x_back[par], in1=ffn[par], op=ALU.add
                                ).then_inc(s_fin, 1)

            def add_halves(q, par):
                for half in range(2):
                    add_second(q, par, range(S // 2 * half, S // 2 * (half + 1)))

            def times_s_add_x(q, par):
                times_s(q, par)
                add_x(q, par)

            def combine_piece(q, n):
                par, m = n // 16, n % 16
                if m in (3, 6):
                    add_second(q, par, range(S // 2 * (m // 6), S // 2 * (m // 6 + 1)))
                elif m == 10:
                    times_s(q, par)
                elif m == 11:
                    add_x(q, par)

            dve.wait_ge(s_dec, 1)
            for b in range(-1, HEAD):
                for n in range(32):
                    mixer_piece(b, n, True)
            for n in range(EARLY):
                mixer_piece(HEAD, n)

            def x_lo(i, par):
                dve.wait_ge(s_fxh, i + 1)
                V.tensor_tensor(out=xhl[:, par, 1, :], in0=banks[XT][:, 0:P],
                                in1=xhl[:, par, 0, :].bitcast(F32), op=ALU.subtract
                                ).then_inc(s_fxl, 1)

            def expert_step(i, k, ends, mix, fin):
                def beside(slot):
                    if beside_slot(mix, 4 * k + slot):
                        mixer_piece(mix, 4 * k + slot)
                    if fin is not None:
                        combine_piece(fin, 4 * k + slot)

                if not ends or i + 1 < TILES:
                    x_lo(i + 1, (k + 1) % 2)
                beside(0)
                if not ends or i < TILES:
                    h = silu_h[:, k % 2, :]
                    dve.wait_ge(s_fs, i + 1)
                    dve.wait_ge(s_fu, i + 1)
                    V.tensor_tensor(out=h, in0=h, in1=banks[UP][:, :], op=ALU.mult
                                    ).then_inc(s_fh, 1)
                beside(1)
                if not ends or 0 <= i - 1 < TILES:
                    par = (k - 1) % 2
                    dve.wait_ge(s_fhh, i)
                    V.tensor_tensor(out=hhl[:, par, 1, :], in0=banks[HT][:, :],
                                    in1=hhl[:, par, 0, :].bitcast(F32), op=ALU.subtract
                                    ).then_inc(s_fhl, 1)
                beside(2)
                if not ends or 0 <= i - 2 < TILES:
                    slot, sub = ((k - 2) // QT) % 2, (k - 2) % QT
                    y = y_quad[:, slot, sub * D:(sub + 1) * D]
                    dve.wait_ge(s_fyh, i - 1)
                    V.tensor_tensor(out=y, in0=y, in1=banks[YP][:, D:2 * D], op=ALU.add
                                    ).then_inc(s_fye, 1)
                beside(3)

            x_lo(0, 0)
            experts_schedule(dve.Fori, expert_step)
            dve.wait_ge(s_s, B)
            with dve.Fori(FIN_IN // 2, B // 2 - 1) as q:
                for piece in (add_halves, times_s_add_x):
                    for par in range(2):
                        piece(q, par)
            q, half_t = B // 2 - 1, T // 2
            add_halves(q, 0)
            times_s_add_x(q, 0)
            for half in range(2):
                add_second(q, 1, range(S // 2 * half, S // 2 * (half + 1)), True)
            for half in range(2):
                part = slice(half * half_t, (half + 1) * half_t)
                s_at = (B - 1) * S * D + half * half_t
                dve.wait_ge(s_fsi, B + half)
                V.tensor_tensor(out=ffn[1][:, part], in0=ffn[1][:, part],
                                in1=xn[:, s_at:s_at + half_t], op=ALU.mult).then_inc(s_f, 1)
            for half in range(2):
                part = slice(half * half_t, (half + 1) * half_t)
                dve.wait_ge(s_f, B + half)
                dve.wait_ge(s_xb[1], 16 * (q + 1))
                V.tensor_tensor(out=x_back[1][:, part], in0=x_back[1][:, part],
                                in1=ffn[1][:, part], op=ALU.add).then_inc(s_fin, 1)

        @block.tensor
        def _(pe):
            mm = nc.tensor.matmul

            def three(out_ps, stat, mov, start, stop):
                mm(out_ps, stat[0], mov[0], start=start, stop=False)
                mm(out_ps, stat[0], mov[1], start=False, stop=False)
                return mm(out_ps, stat[1], mov[0], start=False, stop=stop)

            def norm_step(s, par, first=False):
                pe.wait_ge(s_xnr, s + 1)
                for h in range(2):
                    if not first:
                        pe.wait_ge(s_xte, 2 * s + h - 1)
                    for j in range(S):
                        t = h * S + j
                        last = nc.tensor.transpose(banks[h][:, j * P:(j + 1) * P],
                                                   x_norm[par][:, t * D:(t + 1) * D],
                                                   ident[:, :])
                    last.then_inc(s_xt, 1)
                for h in range(2):
                    pe.wait_ge(s_xte, 2 * s + h + 1)
                    if not first:
                        pe.wait_ge(s_lge, 2 * s + h - 1)
                    for j in range(S):
                        last = mm(banks[2 + h][:, j * E:(j + 1) * E], xn_t[h][:, j * P:(j + 1) * P],
                                  route_w[:, :], start=True, stop=True)
                    last.then_inc(s_lg, 1)

            def count(g):
                gw = SG[g] * E
                pe.wait_ge(s_tri, 4)
                pe.wait_ge(s_pick, g + 1)
                if g:
                    pe.wait_ge(s_place, g)
                mm(counts(g)[0], ones_r, picked[:, 0:gw], start=True, stop=True)
                mm(counts(g)[1], tri, picked[:, 0:gw], start=True, stop=True).then_inc(s_cnt, 1)

            pe.wait_ge(s_const, 2)
            pe.wait_ge(s_params, 16 * 9)
            pe.wait_ge(s_mixraw, 48)
            for n in range(2 * CB):
                last = mm(banks[6][:, n:n + 1], inw_raw[:, n * P:(n + 1) * P], beta_c,
                          start=True, stop=True)
            last.then_inc(s_bmm, 1)
            norm_step(0, 0, True)
            norm_step(1, 1)
            with pe.Fori(1, GROUP_STEPS[0] // 2) as it:
                for par in range(2):
                    norm_step(2 * it + par, par)
            count(0)
            for par in range(2):
                norm_step(NORM_STEPS - 2 + par, par)

            def z_turn(b):
                pe.wait_ge(s_z, S * b + S)
                if past(b, 3):
                    pe.wait_ge(s_s, b - 2)
                elif past(b):
                    pe.wait_ge(s_zl, b)
                for j in range(S):
                    last = nc.tensor.transpose(banks[MC][:, j * P:(j + 1) * P],
                                               z[:, j * D:(j + 1) * D], ident[:, :])
                last.then_inc(s_zt, 1)

            def project(b, c, kind, done):
                n = (kind * CB + c) * P
                three(banks[MA + c][:, :], [inw[:, l, n:n + P] for l in range(2)],
                      [zhl[:, l, :] for l in range(2)], True, True).then_inc(done, 1)

            def project_v(b, c):
                pe.wait_ge(s_zl, b + 1)
                if past(b):
                    if c == 0:
                        pe.wait_ge(s_ge, 2 * b - 1)
                    else:
                        pe.wait_ge(s_gv, 2 * b)
                project(b, c, 1, s_v)

            def project_g(b, c):
                pe.wait_ge(s_ve, 2 * b + c + 1)
                if c == 0 and past(b):
                    pe.wait_ge(s_gv, 2 * b - 1)
                project(b, c, 0, s_g)

            def mix(b, m):
                pe.wait_ge(s_yl, 2 * b + 2)
                if m == 0 and is_batch(b + 1):
                    pe.wait_ge(s_ve, 2 * b + 3)
                else:
                    pe.wait_ge(s_ge, 2 * b + m + 1)
                for c in range(CB):
                    last = three(banks[MA + m][:, :],
                                 [mixw[:, l, c, m * P:(m + 1) * P] for l in range(2)],
                                 [chl[:, l, c, :] for l in range(2)], c == 0, c == CB - 1)
                last.then_inc(s_mx, 1)

            def out_product(b):
                pe.wait_ge(s_gvl, 2 * b + 2)
                if is_batch(b + 2):
                    pe.wait_ge(s_zl, b + 3)
                else:
                    pe.wait_ge(s_s, b)
                for c in range(CB):
                    last = three(banks[MC][:, :], [outw[:, l, c, :] for l in range(2)],
                                 [chl[:, l, c, :] for l in range(2)], c == 0, c == CB - 1)
                last.then_inc(s_o, 1)

            def out_turn(b):
                pe.wait_ge(s_oe, b + 1)
                for j in range(S):
                    last = nc.tensor.transpose(banks[MC][:, j * D:(j + 1) * D],
                                               mixed_t[:, j * P:(j + 1) * P], ident[:, :])
                last.then_inc(s_ot, 1)

            def mixer_piece(b, n):
                if n == 0 and is_batch(b + 1):
                    z_turn(b + 1)
                elif n == 3 and is_batch(b - 1):
                    out_product(b - 1)
                elif n == 5 and is_batch(b - 1):
                    out_turn(b - 1)
                elif n == 6 and is_batch(b + 1):
                    project_v(b + 1, 0)
                elif n in (8, 9) and is_batch(b):
                    mix(b, n - 8)
                elif n == 11 and is_batch(b + 1):
                    project_g(b + 1, 0)
                elif n == 12 and is_batch(b + 1):
                    project_v(b + 1, 1)
                elif n == 14 and is_batch(b + 1):
                    project_g(b + 1, 1)

            mixer_piece(-1, 0)
            count(1)
            pe.wait_ge(s_mws, WEIGHT_STEPS)
            for n in range(1, 16):
                mixer_piece(-1, n)
            for b in range(HEAD):
                for n in range(16):
                    mixer_piece(b, n)
            for n in range(EARLY // 2):
                mixer_piece(HEAD, n)

            def x_turn(i, k, ends):
                slot, sub = (k // QT) % 2, k % QT
                if sub == 0:
                    pe.wait_ge(s_q[slot], 16 * (i // (2 * QT) + 1) if ends
                               else 2 * (i - 4 * slot) + 16)
                if not ends or i >= 1:
                    pe.wait_ge(s_fxl, i)
                nc.tensor.transpose(banks[XT][:, 0:P], x_quad[:, slot, sub * P:(sub + 1) * P],
                                    ident[:, :]).then_inc(s_fx, 1)

            def expert_step(i, k, ends, mix, fin):
                if not ends or i + 1 < TILES:
                    x_turn(i + 1, (k + 1) % 8, ends)
                if not ends or i < TILES:
                    w = pe.snap(expert_of[k % 8], min_val=0, max_val=E - 1) * (4 * HID)
                    pe.wait_ge(s_fxl, i + 1)
                    for half, bank, done, emptied in ((0, GP, s_fg, s_fs), (1, UP, s_fu, s_fh)):
                        if not ends or i >= 1:
                            pe.wait_ge(emptied, i)
                        three(banks[bank][:, :],
                              [xhl[:, k % 2, l, :] for l in range(2)],
                              [gu_w[:, bass.ds(w + l * 2 * HID + half * HID, HID)]
                               for l in range(2)], True, True).then_inc(done, 1)
                if not ends or i + 1 < TILES:
                    pe.reg_load(expert_of[(k + 1) % 8], tile_expert[0:1, bass.ds(i + 1, 1)])
                if beside_slot(mix, 4 * k):
                    mixer_piece(mix, 2 * k)
                if not ends or 0 <= i - 1 < TILES:
                    par = (k - 1) % 2
                    pe.wait_ge(s_fh, i)
                    if not ends or i - 1 >= 1:
                        pe.wait_ge(s_fhl, i - 1)
                    for n in range(HB):
                        last = nc.tensor.transpose(banks[HT][:, n * P:(n + 1) * P],
                                                   silu_h[:, par, n * P:(n + 1) * P], ident[:, :])
                    last.then_inc(s_ft, 1)
                if not ends or 0 <= i - 2 < TILES:
                    par = k % 2
                    w = pe.snap(expert_of[(k - 2) % 8], min_val=0, max_val=E - 1) * (2 * HID)
                    pe.wait_ge(s_fhl, i - 1)
                    if not ends or i - 2 >= 1:
                        pe.wait_ge(s_fye, i - 2)
                    for n in range(HB):
                        wn = w + n * 2 * D
                        mm(banks[YP][:, 0:2 * D], hhl[:, par, 0, n * P:(n + 1) * P],
                           dn_w[:, bass.ds(wn, 2 * D)], start=(n == 0), stop=False)
                        last = mm(banks[YP][:, 0:D], hhl[:, par, 1, n * P:(n + 1) * P],
                                  dn_w[:, bass.ds(wn, D)], start=False, stop=(n == HB - 1))
                    last.then_inc(s_fy, 1)
                if beside_slot(mix, 4 * k + 2):
                    mixer_piece(mix, 2 * k + 1)

            expert_of = [pe.alloc_register(f"expert_of_{k}") for k in range(8)]
            pe.wait_ge(s_wlo, 2 * E)
            pe.wait_ge(s_s, 1)
            pe.reg_load(expert_of[0], tile_expert[0:1, 0:1])
            x_turn(0, 0, True)
            experts_schedule(pe.Fori, expert_step)


_INS = ['L0_attn_x', 'L0_attn_norm_gamma', 'L0_attn_norm_beta', 'L0_attn_in_w', 'L0_attn_in_b',
        'L0_attn_dw_w', 'L0_attn_dw_b', 'L0_attn_log_decay', 'L0_attn_mix_w', 'L0_attn_mix_b',
        'L0_attn_out_w', 'L0_attn_out_b', 'L0_ffn_Wr', 'L0_ffn_Wg', 'L0_ffn_Wu', 'L0_ffn_Wd']


def kernel(**inputs):
    import numpy as _np
    import concourse.bacc as _bacc
    from concourse import mybir as _mybir
    from concourse.bass_utils import run_bass_kernel_spmd as _run

    nc = _bacc.Bacc("TRN2", target_bir_lowering=False, num_devices=1)
    arrays, args = {}, []
    for name in _INS:
        a = _np.ascontiguousarray(inputs[name])
        arrays[f"in_{name}_dram"] = a
        args.append(nc.dram_tensor(f"in_{name}_dram", a.shape, _mybir.dt.from_np(a.dtype),
                                   kind="ExternalInput").ap())
    shape = arrays["in_L0_attn_x_dram"].shape
    args.append(nc.dram_tensor("out_dram", shape, _mybir.dt.float32, kind="ExternalOutput").ap())
    recurrent_moe_block(nc, *args)
    r = _run(nc, [arrays], core_ids=[0])
    return r.results[0]["out_dram"]
```
